# Optimizing a Trainium2 kernel written in Bass

```python
import numpy as np
import jax
import jax.numpy as jnp

def _softmax(x, axis=-1):
    return jax.nn.softmax(x, axis=axis)

def _gelu(x):
    return jax.nn.gelu(x, approximate=True)

def _silu(x):
    return jax.nn.silu(x)

def _sigmoid(x):
    return jax.nn.sigmoid(x)

def _layernorm(x, axis=-1, eps=1e-05):
    m = jnp.mean(x, axis=axis, keepdims=True)
    v = jnp.var(x, axis=axis, keepdims=True)
    return (x - m) / jnp.sqrt(v + eps)

def _scatter_add(tgt, idx, src, axis=0):
    return tgt.at[idx].add(src)

def _segment_sum(src, seg, n):
    return jax.ops.segment_sum(src, seg, n)
kernel_name = 'mk_decoder_postln_d1_seqx_r8_06e968'

def setup_inputs(seed: int=0):
    np.random.seed(seed)
    _w = jnp.asarray

    def _rec_inputs():
        import jax
        import jax.numpy as jnp
        _rk = jax.random.key(seed)
        x = -0.0005207 + 1.001 * jax.random.normal(jax.random.fold_in(_rk, 1), (128, 64, 128), jnp.float32)
        _lenS = 64 - jax.random.randint(jax.random.fold_in(_rk, 7), (128,), 0, max(1, 64 // 4) + 1, jnp.int32)
        _lenS2 = 64 - jax.random.randint(jax.random.fold_in(_rk, 8), (128,), 0, max(1, 64 // 4) + 1, jnp.int32)
        _ctx_512P = jax.random.normal(jax.random.fold_in(_rk, 11), (128, 16, 64), jnp.float32)
        _ctx_512c = jax.random.dirichlet(jax.random.fold_in(_rk, 511), 0.3 * jnp.ones((16,), jnp.float32), (128, 64))
        _ctx_512t = jnp.einsum('bsk,bkd->bsd', _ctx_512c, _ctx_512P)
        _ctx_512t = _ctx_512t * jax.lax.rsqrt(jnp.mean(jnp.square(_ctx_512t)) + 1e-12) * 0.953939
        ctx_512 = 0.502058 + 0.29099 * (_ctx_512t + 0.3 * jax.random.normal(jax.random.fold_in(_rk, 611), (128, 64, 64), jnp.float32))
        itok_BxS2xS_0_7 = jax.random.randint(jax.random.fold_in(_rk, 12), (128, 64, 64), 0, 8, jnp.int32)
        return (x, ctx_512, itok_BxS2xS_0_7)
    x, ctx_512, itok_BxS2xS_0_7 = _rec_inputs()

    def _L0_attn_setup():
        import jax, jax.numpy as jnp
        import numpy as np
        import math
        NUM_HEADS = 16

        def _alibi_bias(L, num_heads):
            slopes = jnp.power(2.0, jnp.linspace(-4.0, -0.3, num_heads))
            pos = jnp.arange(L, dtype=jnp.float32)
            return -(slopes[:, None] * pos[None, :])
        key = jax.random.key(seed)
        ks = jax.random.split(key, 9)
        B, L, D = (2, 256, 128)
        s = 0.02
        return {'x': jax.random.normal(ks[0], (B, L, D), dtype=jnp.float32), 'Wq': jax.random.normal(ks[1], (D, D), dtype=jnp.float32) * s, 'bq': jax.random.normal(ks[2], (D,), dtype=jnp.float32) * s, 'Wk': jax.random.normal(ks[3], (D, D), dtype=jnp.float32) * s, 'bk': jax.random.normal(ks[4], (D,), dtype=jnp.float32) * s, 'Wv': jax.random.normal(ks[5], (D, D), dtype=jnp.float32) * s, 'bv': jax.random.normal(ks[6], (D,), dtype=jnp.float32) * s, 'Wo': jax.random.normal(ks[7], (D, D), dtype=jnp.float32) * s, 'bo': jax.random.normal(ks[8], (D,), dtype=jnp.float32) * s}
    _L0_attn_all = _L0_attn_setup()
    _L0_attn_in = {k: v for k, v in _L0_attn_all.items() if k in ('Wq', 'bq', 'Wk', 'bk', 'Wv', 'bv', 'Wo', 'bo')}
    del _L0_attn_all

    def _L0_xattn_setup():
        import jax, jax.numpy as jnp
        import numpy as np
        key = jax.random.key(seed)
        k1, k2, k3, k4, k5 = jax.random.split(key, 5)
        B, K, S, E, I, D = (4, 2, 64, 8, 128, 256)
        x = jax.random.normal(k1, (B, S, I), dtype=jnp.float32)
        weights = jax.random.uniform(k2, (B, K, S), dtype=jnp.float32)
        ensembles = jax.random.randint(k3, (B, K, S), 0, E, dtype=jnp.int64)
        lim1 = float(np.sqrt(6.0 / (D + I)))
        proj_in = jax.random.uniform(k4, (E, D, I), dtype=jnp.float32, minval=-lim1, maxval=lim1)
        proj_out = jax.random.uniform(k5, (E, I, D), dtype=jnp.float32, minval=-lim1, maxval=lim1)
        return {'x': x, 'weights': weights, 'ensembles': ensembles, 'proj_in': proj_in, 'proj_out': proj_out}
    _L0_xattn_all = _L0_xattn_setup()
    _L0_xattn_in = {k: v for k, v in _L0_xattn_all.items() if k in ('proj_in', 'proj_out')}
    del _L0_xattn_all

    def _L0_ffn_setup():
        import jax, jax.numpy as jnp
        import numpy as np
        NUM_OPS, B, T, D = (8, 8, 64, 128)
        key = jax.random.key(seed)
        k1, k2, k3, k4 = jax.random.split(key, 4)
        x = jax.random.normal(k1, (B, T, D), dtype=jnp.float32)
        W = jax.random.normal(k2, (NUM_OPS, D, D), dtype=jnp.float32) * 0.02
        b = jnp.zeros((NUM_OPS, D), dtype=jnp.float32)
        logits = 0.001 * jax.random.normal(k3, (NUM_OPS,), dtype=jnp.float32)
        u = jax.random.uniform(k4, (NUM_OPS,), dtype=jnp.float32, minval=1e-06, maxval=1.0 - 1e-06)
        return {'x': x, 'W': W, 'b': b, 'logits': logits, 'u': u}
    _L0_ffn_all = _L0_ffn_setup()
    _L0_ffn_in = {k: v for k, v in _L0_ffn_all.items() if k in ('W', 'b', 'logits', 'u')}
    del _L0_ffn_all
    return {'x': x, 'ctx_512': ctx_512, 'itok_BxS2xS_0_7': itok_BxS2xS_0_7, 'L0_attn_Wq': _L0_attn_in['Wq'], 'L0_attn_bq': _L0_attn_in['bq'], 'L0_attn_Wk': _L0_attn_in['Wk'], 'L0_attn_bk': _L0_attn_in['bk'], 'L0_attn_Wv': _L0_attn_in['Wv'], 'L0_attn_bv': _L0_attn_in['bv'], 'L0_attn_Wo': _L0_attn_in['Wo'], 'L0_attn_bo': _L0_attn_in['bo'], 'L0_xattn_proj_in': _L0_xattn_in['proj_in'], 'L0_xattn_proj_out': _L0_xattn_in['proj_out'], 'L0_ffn_W': _L0_ffn_in['W'], 'L0_ffn_b': _L0_ffn_in['b'], 'L0_ffn_logits': _L0_ffn_in['logits'], 'L0_ffn_u': _L0_ffn_in['u']}

def reference(x, ctx_512, itok_BxS2xS_0_7, L0_attn_Wq, L0_attn_bq, L0_attn_Wk, L0_attn_bk, L0_attn_Wv, L0_attn_bv, L0_attn_Wo, L0_attn_bo, L0_xattn_proj_in, L0_xattn_proj_out, L0_ffn_W, L0_ffn_b, L0_ffn_logits, L0_ffn_u):
    import jax
    import jax.numpy as jnp

    def _L0_attn_ref(x, Wq, bq, Wk, bk, Wv, bv, Wo, bo):
        import jax, jax.numpy as jnp
        import numpy as np
        import math
        NUM_HEADS = 16

        def _alibi_bias(L, num_heads):
            slopes = jnp.power(2.0, jnp.linspace(-4.0, -0.3, num_heads))
            pos = jnp.arange(L, dtype=jnp.float32)
            return -(slopes[:, None] * pos[None, :])
        B, L, D = x.shape
        H = NUM_HEADS
        hd = D // H
        scale = math.sqrt(hd)

        def proj(W, b):
            return (jnp.einsum('bld,ed->ble', x, W) + b).reshape(B, L, H, hd)
        q = proj(Wq, bq)
        k = proj(Wk, bk)
        v = proj(Wv, bv)
        scores = jnp.einsum('bqhd,bkhd->bhqk', q, k) / scale
        bias = _alibi_bias(L, H)
        scores = scores + bias[None, :, None, :]
        attn = jax.nn.softmax(scores, axis=-1)
        out = jnp.einsum('bhqk,bkhd->bqhd', attn, v).reshape(B, L, D)
        return jnp.einsum('bld,ed->ble', out, Wo) + bo

    def _L0_xattn_ref(x, weights, ensembles, proj_in, proj_out):
        import jax, jax.numpy as jnp
        import numpy as np
        E = proj_in.shape[0]
        h = jax.nn.relu(jnp.einsum('edi,bsi->bsed', proj_in, x))
        o = jnp.einsum('eid,bsed->bsei', proj_out, h)
        onehot = jax.nn.one_hot(ensembles, E, dtype=x.dtype)
        gate = jnp.einsum('bks,bkse->bse', weights, onehot)
        return jnp.einsum('bsei,bse->bsi', o, gate)

    def _L0_ffn_ref(x, W, b, logits, u):
        import jax, jax.numpy as jnp
        import numpy as np
        NUM_OPS, B, T, D = (8, 8, 64, 128)
        gumbel = -jnp.log(-jnp.log(u))
        idx = jnp.argmax(jax.nn.log_softmax(logits) + gumbel)
        out = jnp.einsum('btd,de->bte', x, W[idx]) + b[idx]
        return out
    x = _layernorm(x + _L0_attn_ref(x, L0_attn_Wq, L0_attn_bq, L0_attn_Wk, L0_attn_bk, L0_attn_Wv, L0_attn_bv, L0_attn_Wo, L0_attn_bo), axis=-1)
    x = _layernorm(x + _L0_xattn_ref(x, ctx_512, itok_BxS2xS_0_7, L0_xattn_proj_in, L0_xattn_proj_out), axis=-1)
    x = _layernorm(x + _L0_ffn_ref(x, L0_ffn_W, L0_ffn_b, L0_ffn_logits, L0_ffn_u), axis=-1)
    return x

_drawn_inputs = setup_inputs


def setup_inputs(seed=0):
    import zlib

    import numpy as np

    out = dict(_drawn_inputs(seed))
    spreads = {'L0_ffn_b': (0.0, 0.1)}
    factors = {'L0_attn_Wq': 8.0,
     'L0_attn_bq': 8.0,
     'L0_attn_Wk': 8.0,
     'L0_attn_bk': 64.0,
     'L0_attn_Wv': 2.909,
     'L0_attn_bv': 8.0,
     'L0_attn_Wo': 2.76,
     'L0_attn_bo': 2.782}
    for name, (base, spread) in spreads.items():
        noise = np.random.default_rng([zlib.crc32(name.encode()), seed]).standard_normal(out[name].shape)
        drawn = base * np.exp(spread * noise) if base else spread * noise
        out[name] = jnp.asarray(drawn.astype(out[name].dtype))
    for name, factor in factors.items():
        out[name] = (out[name] * factor).astype(out[name].dtype)
    return out
```

```python
from contextlib import ExitStack

import concourse.bass as bass
import numpy as np
from concourse import mybir

F32 = mybir.dt.float32
F32R = mybir.dt.float32r
F16 = mybir.dt.float16
I32 = mybir.dt.int32
ALU = mybir.AluOpType
ACT = mybir.ActivationFunctionType
AX = mybir.AxisListType

P = 128
B, L, D = 128, 64, 128
H, HD = 16, 8
E, DH = 8, 256
K = 64
NOPS = 8
BLK = 512
NB = B * L // BLK
NT = BLK // P
NC = E * DH // P
NG, HG = 4, 4
TERM = HG * HD
ROWS = 3 * TERM
MROWS = ROWS + 2
MAXSCALE = 256.0
VC = 2 * 2 * (HD + 1)
EPS = 1e-5
SCALE = float(1.0 / np.sqrt(HD))
SLOTS = NC
GATE_SLOTS = {3: (0,), 5: (1,), 10: (2,), 11: (3,), 12: (4,), 13: (5,), 14: (6,), 15: (7,)}
KHEAD_SLOTS = {9: (0,), 10: (1, 2), 11: (3,), 12: (4, 5), 13: (6,), 14: (7,)}
QHEAD_SLOTS = {3: (0,), 4: (1,), 5: (2, 3)}


class Step:

    def __init__(self, t, i, u):
        self.t, self.i, self.u = t, i, u
        fixed = isinstance(t, int)
        self.project = not fixed or 0 <= t + 2 < NB
        self.attend = not fixed or 0 <= t + 1 < NB
        self.experts = not fixed or 0 <= t < NB
        self.finish = not fixed or 0 <= t - 1 < NB
        self.pb, self.pu, self.ph = t + 2, u, i + 1
        self.ab, self.au, self.ah = t + 1, 1 - u, i + u
        self.eb, self.eu = t, u
        self.fb, self.fu, self.fh = t - 1, 1 - u, i - 1 + u


def pipeline(eng, run):
    for t in range(-2, 3):
        run(Step(t, t // 2, t % 2))
    with eng.Fori(1, NB // 2 - 2) as i:
        run(Step(2 * i + 1, i, 1))
        run(Step(2 * i + 2, i + 1, 0))
    for t in range(NB - 3, NB + 1):
        run(Step(t, t // 2, t % 2))


def need(eng, sem, value):
    if isinstance(value, int) and value <= 0:
        return
    eng.wait_ge(sem, value)


def decoder_layer(nc, x_tok, x_t, gate_w, gate_e, wq_t, bq, wk_t, bk, wv_t, bv, wo_t, bo,
                  w_in, w_out, ffn_w, ffn_b, logits, u, ident_c, decay_c, headmask_c, iota_c, out):
    ctx = ExitStack()
    with ctx:
        def sb(name, shape, dt=F32):
            return ctx.enter_context(nc.sbuf_tensor(name, shape, dt))

        def sem(name):
            return ctx.enter_context(nc.semaphore(name))

        ident = sb("ident", [P, P])
        decay = sb("decay", [P, H])
        headmask = sb("headmask", [P, HG])
        iota = sb("iota", [P, NOPS])
        wq = sb("wq", [P, D])
        wk = sb("wk", [P, D])
        wv = sb("wv", [P, D])
        wo = sb("wo", [P, D])
        bqs = sb("bqs", [P, 1])
        bks = sb("bks", [P, 1])
        bvs = sb("bvs", [P, 1])
        bos = sb("bos", [P, D])
        attn_bias = sb("attn_bias", [P, D])
        win_h = sb("win_h", [P, NC * P], F32R)
        win_l = sb("win_l", [P, NC * P], F32R)
        wout = sb("wout", [P, NC, D])
        ffw = sb("ffw", [P, D])
        ffb = sb("ffb", [P, D])
        xt = sb("xt", [P, 2, BLK])
        xtok = sb("xtok", [P, 2, NT, D])
        gw = sb("gw", [P, 2, NT, K])
        ge = sb("ge", [P, 2, NT, K], I32)
        qh = sb("qh", [P, BLK], F16)
        ql = sb("ql", [P, BLK], F16)
        kh = sb("kh", [P, BLK], F16)
        kl = sb("kl", [P, BLK], F16)
        q_stack = sb("q_stack", [P, 2, NG, BLK], F16)
        k_stack = sb("k_stack", [P, 2, NG, BLK], F16)
        k_heads = sb("k_heads", [P, NG, HG, BLK], F16)
        q_heads = sb("q_heads", [P, NG, HG, BLK], F16)
        smax = sb("smax", [P, NT, H])
        mh = sb("mh", [H, BLK], F16)
        ml = sb("ml", [H, BLK], F16)
        probs = sb("probs", [P, 2, H // 2, 2, L])
        vals = sb("vals", [P, 2, NT, H // 2, VC])
        rden = sb("rden", [P, H // 2, 4])
        o_tok = sb("o_tok", [P, NT, D])
        o_t = sb("o_t", [P, BLK])
        xb = sb("xb", [P, NT, D])
        picked = sb("picked", [P, E, NT, K])
        gate = sb("gate", [P, 2, E, NT])
        gates = sb("gates", [P, 2, E, BLK])
        x1 = sb("x1", [P, 2, NT, D])
        x1h = sb("x1h", [P, 2, BLK], F32R)
        x1l = sb("x1l", [P, 2, BLK], F32R)
        hid = sb("hid", [P, 2, BLK])
        moe_t = sb("moe_t", [P, BLK])
        x2 = sb("x2", [P, NT, D])
        x2b = sb("x2b", [P, NT, D])
        x2_t = sb("x2_t", [P, BLK])
        y = sb("y", [P, 2, NT, D])
        ln_x = sb("ln_x", [P, 3, NT, D])
        ln_st = sb("ln_st", [P, 3, NT, 6])
        ln_mv = sb("ln_mv", [P, 3, NT, 2])
        ln_ve = sb("ln_ve", [P, 3, NT])
        ln_rs = sb("ln_rs", [P, 3, NT])
        minus_half = sb("minus_half", [P, NT])
        win_raw = sb("win_raw", [P, NC * P // 2])
        choice = sb("choice", [P, 12, NOPS])
        pick = sb("pick", [P, 8])

        def bank(name, cols=512):
            return ctx.enter_context(nc.psum_tensor(name, [P, cols], F32))

        ps_hid = [bank("ps_hid0"), bank("ps_hid1")]
        ps_moe = bank("ps_moe")
        ps_score = [bank("ps_score0"), bank("ps_score1")]
        ps_pf = bank("ps_pf")
        ps_at = bank("ps_at")
        ps_gate = bank("ps_gate")

        s_const = sem("s_const")
        s_win = [sem("s_win0"), sem("s_win1")]
        s_set = sem("s_set")
        s_seta = sem("s_seta")
        s_setp = sem("s_setp")
        s_sett = sem("s_sett")
        ld_xt = [sem("ld_xt0"), sem("ld_xt1")]
        ld_xtok = [sem("ld_xtok0"), sem("ld_xtok1")]
        ld_gate = [sem("ld_gate0"), sem("ld_gate1")]
        pe_q, pe_k, pe_v = sem("pe_q"), sem("pe_k"), sem("pe_v")
        qh_done, ql_done, kh_done, kl_done = sem("qh_done"), sem("ql_done"), sem("kh_done"), sem("kl_done")
        vals_done = sem("vals_done")
        kstack_in, qstack_in = sem("kstack_in"), sem("qstack_in")
        kheads_done, qheads_done = sem("kheads_done"), sem("qheads_done")
        pe_score = sem("pe_score")
        max_done = sem("max_done")
        pe_maxt = sem("pe_maxt")
        mh_done, ml_done = sem("mh_done"), sem("ml_done")
        max_in = sem("max_in")
        pe_logit = sem("pe_logit")
        exp_done = sem("exp_done")
        pe_pv = sem("pe_pv")
        rden_done = sem("rden_done")
        otok_done = sem("otok_done")
        pe_ot, ot_done, pe_op = sem("pe_ot"), sem("ot_done"), sem("pe_op")
        xb_done = sem("xb_done")
        eq_done = sem("eq_done")
        picked_done = sem("picked_done")
        tree_done = sem("tree_done")
        gate_done = sem("gate_done")
        pe_gate = sem("pe_gate")
        gates_done = sem("gates_done")
        ln_sum = [sem(f"ln_sum{n}") for n in range(3)]
        ln_stat = [sem(f"ln_stat{n}") for n in range(3)]
        ln_var = [sem(f"ln_var{n}") for n in range(3)]
        ln_eps = [sem(f"ln_eps{n}") for n in range(3)]
        ln_rstd = [sem(f"ln_rstd{n}") for n in range(3)]
        ln_out = [sem(f"ln_out{n}") for n in range(3)]
        pe_x1t, x1h_done, x1l_done = sem("pe_x1t"), sem("x1h_done"), sem("x1l_done")
        pe_hid, hid_done, pe_moe = sem("pe_hid"), sem("hid_done"), sem("pe_moe")
        moe_done, pe_moet = sem("moe_done"), sem("pe_moet")
        pe_x2t, x2t_done, x2b_done, pe_ffn = sem("pe_x2t"), sem("x2t_done"), sem("x2b_done"), sem("pe_ffn")
        stored = [sem("stored0"), sem("stored1")]

        consts = [(ident, ident_c), (decay, decay_c), (headmask, headmask_c), (iota, iota_c),
                  (wq, wq_t), (wk, wk_t), (wv, wv_t), (wo, wo_t),
                  (bqs, bq), (bks, bk), (bvs, bv), (wout, w_out)]
        WH = NC * P // 2
        ffw_all = gates[:, 0, :, 0:D]
        ffb_all = gates[:, 1, :, 0:D]
        vals_v = vals[:].rearrange("p u j m (h b x) -> p u j b h m x", h=2, b=2)

        block = ctx.enter_context(nc.Block())

        @block.sync
        def _(sp):
            for dst, src in consts:
                sp.dma_start(dst[:], src).then_inc(s_const, 16)
            sp.dma_start(bos[:], bo.broadcast_to([P, D])).then_inc(s_const, 16)
            sp.dma_start(choice[:, 0, :], logits.broadcast_to([P, NOPS])).then_inc(s_const, 16)
            sp.dma_start(choice[:, 1, :], u.broadcast_to([P, NOPS])).then_inc(s_const, 16)
            sp.dma_start(ffw_all, ffn_w).then_inc(s_const, 16)
            for n in range(NOPS):
                sp.dma_start(ffb_all[:, n, :], ffn_b[n:n + 1, :].broadcast_to([P, D])).then_inc(s_const, 16)
            sp.dma_start(win_raw[:], w_in[:, 0:WH]).then_inc(s_win[0], 16)
            for b in range(2):
                sp.dma_start(xt[:, b, :], x_t[b]).then_inc(ld_xt[b], 16)
                sp.dma_start(gw[:, b, :, :], gate_w[b]).then_inc(ld_gate[b], 16)
                sp.dma_start(ge[:, b, :, :], gate_e[b]).then_inc(ld_gate[b], 16)
                sp.dma_start(xtok[:, b, :, :], x_tok[b]).then_inc(ld_xtok[b], 16)
            need(sp, s_set, 2)
            sp.dma_start(win_raw[:], w_in[:, WH:]).then_inc(s_win[1], 16)

            def step(s):
                fixed = isinstance(s.t, int)
                if not fixed or 2 <= s.t + 3 < NB:
                    need(sp, pe_v, s.pb)
                    sp.dma_start(xt[:, s.au, :], x_t[s.t + 3]).then_inc(ld_xt[s.au], 16)
                    need(sp, picked_done, E * s.pb)
                    sp.dma_start(gw[:, s.au, :, :], gate_w[s.t + 3]).then_inc(ld_gate[s.au], 16)
                    sp.dma_start(ge[:, s.au, :, :], gate_e[s.t + 3]).then_inc(ld_gate[s.au], 16)
                if not fixed or 2 <= s.t + 2 < NB:
                    need(sp, xb_done, s.ab)
                    sp.dma_start(xtok[:, s.u, :, :], x_tok[s.t + 2]).then_inc(ld_xtok[s.u], 16)
                if s.project:
                    need(sp, kl_done, s.pb + 1)
                    for n, src in enumerate((kh, kh, kl)):
                        for g in range(NG):
                            sp.dma_start(k_stack[TERM * n:TERM * (n + 1), s.pu, g, :],
                                         src[TERM * g:TERM * (g + 1), :]).then_inc(kstack_in, 16)
                if s.attend:
                    need(sp, ml_done, s.ab + 1)
                    for n, src in enumerate((mh, ml)):
                        sp.dma_start(q_heads[ROWS + n:ROWS + n + 1, :, :, :].rearrange("o g h c -> o (g h) c"),
                                     src[:, :]).then_inc(max_in, 16)
                if s.project:
                    need(sp, ql_done, s.pb + 1)
                    for n, src in enumerate((qh, ql, qh)):
                        for g in range(NG):
                            sp.dma_start(q_stack[TERM * n:TERM * (n + 1), s.pu, g, :],
                                         src[TERM * g:TERM * (g + 1), :]).then_inc(qstack_in, 16)
                if s.finish:
                    need(sp, ln_out[2], s.fb + 1)
                    sp.dma_start(out[s.fb], y[:, s.fu, :, :]).then_inc(stored[s.fu], 16)

            pipeline(sp, step)
            for n in range(2):
                sp.wait_ge(stored[n], 16 * (NB // 2))

        @block.gpsimd
        def _(pool):
            nc.gpsimd.memset(minus_half[:], -0.5).then_inc(s_setp, 1)
            nc.gpsimd.memset(vals[:], 0.0).then_inc(s_setp, 1)
            pool.wait_ge(s_setp, 2)

            def rstd(n, b):
                need(pool, ln_eps[n], b + 1)
                nc.gpsimd.tensor_tensor(ln_rs[:, n, :], ln_ve[:, n, :], minus_half[:], ALU.pow).then_inc(ln_rstd[n], 1)

            def pick_expert(s, e):
                nc.gpsimd.tensor_scalar(picked[:, e, :, :], ge[:, s.pu, :, :], float(e), None, ALU.is_equal).then_inc(eq_done, 1)
                need(pool, eq_done, E * s.pb + e + 1)
                nc.gpsimd.tensor_tensor(picked[:, e, :, :], picked[:, e, :, :], gw[:, s.pu, :, :], ALU.mult).then_inc(picked_done, 1)

            def sum_gates(s):
                need(pool, picked_done, E * (s.pb + 1))
                pk = picked[:].rearrange("p e j k -> p (e j) k")
                w = K // 2
                n = 0
                while w > 1:
                    if n:
                        need(pool, tree_done, 5 * s.pb + n)
                    nc.gpsimd.tensor_tensor(pk[:, :, 0:w], pk[:, :, 0:w], pk[:, :, w:2 * w], ALU.add).then_inc(tree_done, 1)
                    w //= 2
                    n += 1
                need(pool, tree_done, 5 * s.pb + 5)
                need(pool, pe_gate, E * (s.pb - 1))
                nc.gpsimd.tensor_tensor(gate[:, s.pu, :, :].rearrange("p e j -> p (e j)").unsqueeze(2),
                                        pk[:, :, 0:1], pk[:, :, 1:2], ALU.add).then_inc(gate_done, 1)

            def step(s):
                if s.project:
                    need(pool, gate_done, s.pb)
                    need(pool, ld_gate[s.pu], 32 * s.ph + 32)
                if s.attend:
                    if isinstance(s.t, int) and s.t == -1:
                        pool.wait_ge(s_set, 4)
                    need(pool, ld_xtok[s.au], 16 * s.ah + 16)
                    need(pool, ln_sum[0], s.ab)
                    nc.gpsimd.tensor_tensor(xb[:], xtok[:, s.au, :, :],
                                            attn_bias[:].unsqueeze(1).broadcast_to([P, NT, D]), ALU.add).then_inc(xb_done, 1)
                if s.project:
                    for e in range(2):
                        pick_expert(s, e)
                if s.finish:
                    rstd(1, s.fb)
                if s.project:
                    for e in range(2, 4):
                        pick_expert(s, e)
                if s.finish:
                    need(pool, ln_out[1], s.fb + 1)
                    need(pool, ln_sum[2], s.fb)
                    nc.gpsimd.tensor_tensor(x2b[:], x2[:], ffb[:].unsqueeze(1).broadcast_to([P, NT, D]),
                                            ALU.add).then_inc(x2b_done, 1)
                if s.project:
                    for e in range(4, 6):
                        pick_expert(s, e)
                if s.finish:
                    rstd(2, s.fb)
                if s.project:
                    for e in range(6, 8):
                        pick_expert(s, e)
                    sum_gates(s)
                if s.attend:
                    rstd(0, s.ab)

            pipeline(pool, step)

        @block.scalar
        def _(act):
            act.wait_ge(s_win[0], 16)
            nc.scalar.activation(win_h[:, 0:WH], win_raw[:], ACT.Copy).then_inc(s_seta, 1)
            act.wait_ge(s_set, 2)
            act.wait_ge(s_win[1], 16)
            nc.scalar.activation(win_h[:, WH:], win_raw[:], ACT.Copy).then_inc(s_seta, 1)
            act.wait_ge(s_set, 6)
            nc.scalar.activation(choice[:, 3, :], choice[:, 2, :], ACT.Exp, accum_out=pick[:, 1:2]).then_inc(s_seta, 1)
            act.wait_ge(s_seta, 3)
            nc.scalar.activation(pick[:, 2:3], pick[:, 1:2], ACT.Ln).then_inc(s_seta, 1)
            nc.scalar.activation(choice[:, 4, :], choice[:, 1, :], ACT.Ln).then_inc(s_seta, 1)
            act.wait_ge(s_seta, 5)
            nc.scalar.activation(choice[:, 5, :], choice[:, 4, :], ACT.Ln, scale=-1.0).then_inc(s_seta, 1)

            def high(psum, dst, bias, full, free, b, done):
                need(act, full, b + 1)
                need(act, free, 192 * b)
                nc.scalar.activation(dst[:], psum[:], ACT.Identity, bias=bias[:, 0:1]).then_inc(done, 1)

            def keep_gate(s, e):
                need(act, pe_gate, E * s.ab + e + 1)
                if e == 0:
                    need(act, hid_done, NC * (s.ab - 1))
                nc.scalar.activation(gates[:, s.au, e, :], ps_gate[:], ACT.Copy).then_inc(gates_done, 1)

            def exps(s, j):
                need(act, pe_logit, 8 * s.ab + j + 1)
                if j % 2 == 0:
                    need(act, pe_pv, NT * s.ab + j // 2 - 1)
                nc.scalar.activation(probs[:, j // 2 % 2, :, j % 2, :], ps_score[j % 2][:].rearrange("p (m q) -> p m q", q=L),
                                     ACT.Exp, scale=SCALE).then_inc(exp_done, 1)

            def k_head(s, n):
                h, g = n // 2, slice(2 * (n % 2), 2 * (n % 2) + 2)
                if n == 0:
                    need(act, kstack_in, 192 * (s.pb + 1))
                    need(act, pe_score, 8 * s.pb)
                ins = nc.scalar.activation(k_heads[0:ROWS, g, h, :], k_stack[0:ROWS, s.pu, g, :], ACT.Copy,
                                           scale=headmask[0:ROWS, h:h + 1])
                if n == 2 * HG - 1:
                    ins.then_inc(kheads_done, 1)

            def step(s):
                if s.finish:
                    need(act, pe_moe, NC * (s.fb + 1))
                    need(act, pe_moet, s.fb)
                    nc.scalar.activation(moe_t[:], ps_moe[:], ACT.Copy).then_inc(moe_done, 1)
                if s.project:
                    high(ps_pf, qh, bqs, pe_q, qstack_in, s.pb, qh_done)
                for c in range(SLOTS):
                    if s.project and c == 1:
                        high(ps_pf, kh, bks, pe_k, kstack_in, s.pb, kh_done)
                    if s.attend and c == 4:
                        need(act, pe_maxt, s.ab + 1)
                        need(act, max_in, 32 * s.ab)
                        nc.scalar.activation(mh[:], ps_at[0:H, :], ACT.Copy, scale=1.0 / MAXSCALE).then_inc(mh_done, 1)
                    if s.finish and c == 5:
                        need(act, pe_x2t, s.fb + 1)
                        need(act, pe_ffn, s.fb)
                        nc.scalar.activation(x2_t[:], ps_pf[:], ACT.Copy).then_inc(x2t_done, 1)
                    if s.attend and 6 <= c < 10:
                        exps(s, 2 * (c - 6))
                        exps(s, 2 * (c - 6) + 1)
                    if s.attend and c == 11:
                        need(act, pe_ot, s.ab + 1)
                        need(act, pe_op, s.ab)
                        nc.scalar.activation(o_t[:], ps_at[:], ACT.Copy).then_inc(ot_done, 1)
                    if s.attend:
                        for e in GATE_SLOTS.get(c, ()):
                            keep_gate(s, e)
                    if s.project:
                        for n in KHEAD_SLOTS.get(c, ()):
                            k_head(s, n)
                    if s.attend and c == 15:
                        need(act, pe_x1t, s.ab + 1)
                        nc.scalar.activation(x1h[:, s.au, :], ps_at[:], ACT.Copy).then_inc(x1h_done, 1)

            pipeline(act, step)

        @block.vector
        def _(dve):
            count = [0]

            def did(ins):
                count[0] += 1
                ins.then_inc(s_set, 1)
                dve.wait_ge(s_set, count[0])

            nc.vector.memset(k_stack[ROWS:MROWS, :, :, :], -MAXSCALE)
            dve.wait_ge(s_seta, 1)
            did(nc.vector.tensor_tensor(win_l[:, 0:WH], win_raw[:], win_h[:, 0:WH].bitcast(F32), ALU.subtract))
            did(nc.vector.memset(pick[:], 0.0))
            dve.wait_ge(s_seta, 2)
            did(nc.vector.tensor_tensor(win_l[:, WH:], win_raw[:], win_h[:, WH:].bitcast(F32), ALU.subtract))
            dve.wait_ge(s_const, 16 * (len(consts) + 4 + NOPS))
            dve.wait_ge(s_sett, 1)
            did(nc.vector.tensor_tensor(attn_bias[:], ps_at[:, 0:D], bos[:], ALU.add))
            did(nc.vector.tensor_reduce(pick[:, 0:1], choice[:, 0, :], AX.X, ALU.max))
            did(nc.vector.tensor_scalar(choice[:, 2, :], choice[:, 0, :], pick[:, 0:1], None, ALU.subtract))
            dve.wait_ge(s_seta, 6)
            did(nc.vector.tensor_scalar(choice[:, 6, :], choice[:, 2, :], pick[:, 2:3], None, ALU.subtract))
            did(nc.vector.tensor_tensor(choice[:, 7, :], choice[:, 6, :], choice[:, 5, :], ALU.subtract))
            did(nc.vector.tensor_reduce(pick[:, 3:4], choice[:, 7, :], AX.X, ALU.max))
            did(nc.vector.tensor_scalar(choice[:, 8, :], choice[:, 7, :], pick[:, 3:4], float(NOPS), ALU.is_lt, ALU.mult))
            did(nc.vector.tensor_tensor(choice[:, 9, :], choice[:, 8, :], iota[:], ALU.add))
            did(nc.vector.tensor_reduce(pick[:, 4:5], choice[:, 9, :], AX.X, ALU.min))
            did(nc.vector.tensor_scalar(choice[:, 10, :], iota[:], pick[:, 4:5], None, ALU.is_equal))
            for dst, src in ((ffw, ffw_all), (ffb, ffb_all)):
                did(nc.vector.tensor_scalar(dst[:], src[:, 0, :], choice[:, 10, 0:1], None, ALU.mult))
                for n in range(1, NOPS):
                    did(nc.vector.scalar_tensor_tensor(out=dst[:], in0=src[:, n, :], scalar=choice[:, 10, n:n + 1],
                                                       in1=dst[:], op0=ALU.mult, op1=ALU.add))
            dve.wait_ge(s_setp, 2)
            dec = decay[:].rearrange("p (h m) -> p h m", h=2)
            for par in range(2):
                for j in range(NT):
                    for b in range(2):
                        r = slice(L * b, L * b + L)
                        last = nc.vector.tensor_copy(vals_v[r, par, j, b, :, :, HD], dec[r])
            did(last)

            def low(psum, dst, high, bias, ready, b, done):
                need(dve, ready, b + 1)
                nc.vector.scalar_tensor_tensor(out=dst[:], in0=psum[:], scalar=bias[:, 0:1], in1=high[:],
                                               op0=ALU.add, op1=ALU.subtract).then_inc(done, 1)

            def keep_vals(s):
                need(dve, pe_v, s.pb + 1)
                need(dve, pe_pv, NT * (s.pb - 1))
                for j in range(NT):
                    v = ps_pf[:, P * j:P * (j + 1)].rearrange("p (h m x) -> p h m x", h=2, x=HD)
                    for b in range(2):
                        r = slice(L * b, L * b + L)
                        last = nc.vector.tensor_tensor(vals_v[r, s.pu, j, b, :, :, 0:HD], v[r],
                                                       dec[r].unsqueeze(3).broadcast_to([L, 2, H // 2, HD]), ALU.mult)
                last.then_inc(vals_done, 1)

            def maximum(s, j):
                need(dve, pe_score, 8 * s.ab + j + 1)
                if j == 0:
                    need(dve, pe_maxt, s.ab)
                nc.vector.tensor_reduce(smax[:, j // 2, 8 * (j % 2):8 * (j % 2) + 8],
                                        ps_score[j % 2][:].rearrange("p (h k) -> p h k", k=L), AX.X,
                                        ALU.max).then_inc(max_done, 1)

            def normalise(s, j):
                need(dve, pe_pv, NT * s.ab + j + 1)
                acc = ps_at[:, 0:H // 2 * VC].rearrange("p (m q x) -> p m q x", q=4, x=HD + 1)
                nc.vector.reciprocal(rden[:], acc[:, :, :, HD]).then_inc(rden_done, 1)
                if j == 0:
                    need(dve, pe_ot, s.ab)
                need(dve, rden_done, NT * s.ab + j + 1)
                for h2 in range(2):
                    for b in range(2):
                        q = 2 * h2 + b
                        r = slice(L * h2, L * h2 + L)
                        dst = o_tok[L * b:L * b + L, j, 64 * h2:64 * h2 + 64].rearrange("p (m x) -> p m x", x=HD)
                        last = nc.vector.tensor_tensor(dst, acc[r, :, q, 0:HD],
                                                       rden[r, :, q].unsqueeze(2).broadcast_to([L, H // 2, HD]), ALU.mult)
                last.then_inc(otok_done, 1)

            def q_head(s, h):
                if h == 0:
                    need(dve, qstack_in, 192 * (s.ab + 1))
                    need(dve, pe_logit, 8 * s.ab)
                ins = nc.vector.tensor_scalar(q_heads[0:ROWS, :, h, :], q_stack[0:ROWS, s.au, :, :],
                                              headmask[0:ROWS, h:h + 1], None, ALU.mult)
                if h == HG - 1:
                    ins.then_inc(qheads_done, 1)

            def stats(n, b):
                need(dve, ln_sum[n], b + 1)
                for j in range(NT):
                    last = nc.vector.bn_stats(ln_st[:, n, j, :], ln_x[:, n, j, :])
                last.then_inc(ln_stat[n], 1)

            def variance(n, b):
                for j in range(NT):
                    last = nc.vector.bn_aggr(ln_mv[:, n, j, :], ln_st[:, n, j, :])
                last.then_inc(ln_var[n], 1)

            def add_eps(n, b):
                need(dve, ln_var[n], b + 1)
                nc.vector.tensor_scalar(ln_ve[:, n, :], ln_mv[:, n, :, 1], EPS, None, ALU.add).then_inc(ln_eps[n], 1)

            def scale_out(n, b, dst):
                need(dve, ln_rstd[n], b + 1)
                for j in range(NT):
                    last = nc.vector.tensor_scalar(dst[:, j, :], ln_x[:, n, j, :], ln_mv[:, n, j, 0:1],
                                                   ln_rs[:, n, j:j + 1], ALU.subtract, ALU.mult)
                last.then_inc(ln_out[n], 1)

            def step(s):
                if s.attend:
                    maximum(s, 0)
                    maximum(s, 1)
                if s.project:
                    low(ps_pf, ql, qh, bqs, qh_done, s.pb, ql_done)
                if s.finish:
                    need(dve, pe_moet, s.fb + 1)
                    nc.vector.tensor_tensor(ln_x[:, 1, :, :], ps_gate[:].rearrange("p (j d) -> p j d", d=D),
                                            x1[:, s.fu, :, :], ALU.add).then_inc(ln_sum[1], 1)
                for c in range(SLOTS):
                    if s.finish and c == 2:
                        need(dve, ln_stat[1], s.fb + 1)
                    if s.finish and c == 10:
                        need(dve, ln_stat[2], s.fb + 1)
                    if s.attend and c == 13:
                        need(dve, ln_stat[0], s.ab + 1)
                    if s.experts:
                        need(dve, pe_hid, NC * s.eb + c + 1)
                        if c % 2 == 0:
                            need(dve, gates_done, E * s.eb + c // 2 + 1)
                        need(dve, pe_moe, NC * s.eb + c - 1)
                        nc.vector.scalar_tensor_tensor(out=hid[:, c % 2, :], in0=ps_hid[c % 2][:], scalar=0.0,
                                                       in1=gates[:, s.eu, c // 2, :], op0=ALU.max,
                                                       op1=ALU.mult).then_inc(hid_done, 1)
                    if s.attend and c == 0:
                        maximum(s, 2)
                        maximum(s, 3)
                    if s.finish and c == 0:
                        stats(1, s.fb)
                    if s.project and c == 1:
                        low(ps_pf, kl, kh, bks, kh_done, s.pb, kl_done)
                    if s.attend and c == 1:
                        maximum(s, 4)
                    if s.finish and c == 2:
                        variance(1, s.fb)
                    if s.attend and c == 2:
                        maximum(s, 5)
                    if s.finish and c == 2:
                        add_eps(1, s.fb)
                    if s.attend and c == 2:
                        maximum(s, 6)
                    if s.attend and c == 3:
                        maximum(s, 7)
                    if s.finish and c == 4:
                        scale_out(1, s.fb, x2)
                    if s.attend and c == 4:
                        need(dve, mh_done, s.ab + 1)
                        nc.vector.scalar_tensor_tensor(out=ml[:], in0=ps_at[0:H, :], scalar=1.0 / MAXSCALE, in1=mh[:],
                                                       op0=ALU.mult, op1=ALU.subtract).then_inc(ml_done, 1)
                    if s.attend:
                        for h in QHEAD_SLOTS.get(c, ()):
                            q_head(s, h)
                    if s.attend and 7 <= c < 11:
                        normalise(s, c - 7)
                    if s.finish and c == 8:
                        need(dve, pe_ffn, s.fb + 1)
                        need(dve, x2b_done, s.fb + 1)
                        nc.vector.tensor_tensor(ln_x[:, 2, :, :], ps_pf[:].rearrange("p (j d) -> p j d", d=D),
                                                x2b[:], ALU.add).then_inc(ln_sum[2], 1)
                    if s.finish and c == 9:
                        stats(2, s.fb)
                    if s.finish and c == 10:
                        variance(2, s.fb)
                        add_eps(2, s.fb)
                    if s.project and c == 11:
                        keep_vals(s)
                    if s.attend and c == 12:
                        need(dve, pe_op, s.ab + 1)
                        need(dve, xb_done, s.ab + 1)
                        nc.vector.tensor_tensor(ln_x[:, 0, :, :], ps_at[:].rearrange("p (j d) -> p j d", d=D),
                                                xb[:], ALU.add).then_inc(ln_sum[0], 1)
                        stats(0, s.ab)
                    if s.attend and c == 13:
                        variance(0, s.ab)
                        add_eps(0, s.ab)
                    if s.finish and c == 13:
                        need(dve, stored[s.fu], 16 * s.fh)
                        scale_out(2, s.fb, y[:, s.fu, :, :])
                    if s.attend and c == 15:
                        scale_out(0, s.ab, x1[:, s.au, :, :])
                        need(dve, x1h_done, s.ab + 1)
                        nc.vector.tensor_tensor(x1l[:, s.au, :], ps_at[:], x1h[:, s.au, :].bitcast(F32),
                                                ALU.subtract).then_inc(x1l_done, 1)

            pipeline(dve, step)

        @block.tensor
        def _(pe):
            pe.wait_ge(s_const, 16 * (len(consts) + 4 + NOPS))
            nc.tensor.matmul(ps_at[:, 0:D], bvs[:, 0:1].broadcast_to([P, P]), wo[:], start=True, stop=True).then_inc(s_sett, 1)
            pe.wait_ge(s_set, 4)

            def hidden(s, c):
                if c == 0:
                    need(pe, x1h_done, s.eb + 1)
                    need(pe, x1l_done, s.eb + 1)
                need(pe, hid_done, NC * s.eb + c - 1)
                w = slice(P * c, P * (c + 1))
                nc.tensor.matmul(ps_hid[c % 2][:], win_h[:, w], x1h[:, s.eu, :], start=True, stop=False)
                nc.tensor.matmul(ps_hid[c % 2][:], win_l[:, w], x1h[:, s.eu, :], start=False, stop=False)
                nc.tensor.matmul(ps_hid[c % 2][:], win_h[:, w], x1l[:, s.eu, :], start=False, stop=True).then_inc(pe_hid, 1)

            def expert_out(s, c):
                need(pe, hid_done, NC * s.eb + c + 1)
                if c == 0:
                    need(pe, moe_done, s.eb)
                nc.tensor.matmul(ps_moe[:], wout[:, c, :], hid[:, c % 2, :], start=(c == 0),
                                 stop=(c == NC - 1)).then_inc(pe_moe, 1)

            def tiles_t(dst, src, done):
                for j in range(NT):
                    last = nc.tensor.transpose(dst[:, P * j:P * (j + 1)], src(j), ident[:])
                last.then_inc(done, 1)

            def score(s, j):
                if j == 0:
                    need(pe, kheads_done, s.ab + 1)
                    need(pe, qstack_in, 192 * (s.ab + 1))
                if j < 2:
                    need(pe, exp_done, 8 * s.ab - 1 + j)
                else:
                    need(pe, max_done, 8 * s.ab + j - 1)
                for g in (2 * (j % 2), 2 * (j % 2) + 1):
                    for b in range(2):
                        tok = slice(P * (j // 2) + L * b, P * (j // 2) + L * b + L)
                        last = nc.tensor.matmul(ps_score[j % 2][L * b:L * b + L, 256 * (g % 2):256 * (g % 2) + 256],
                                                q_stack[0:ROWS, s.au, g, tok], k_heads[0:ROWS, g, :, tok],
                                                start=True, stop=True)
                last.then_inc(pe_score, 1)

            def logit(s, j):
                if j == 0:
                    need(pe, max_in, 32 * (s.ab + 1))
                    need(pe, qheads_done, s.ab + 1)
                if j < 2:
                    need(pe, max_done, 8 * s.ab + 7 + j)
                else:
                    need(pe, exp_done, 8 * s.ab + j - 1)
                for g in (2 * (j % 2), 2 * (j % 2) + 1):
                    for b in range(2):
                        tok = slice(P * (j // 2) + L * b, P * (j // 2) + L * b + L)
                        last = nc.tensor.matmul(ps_score[j % 2][L * b:L * b + L, 256 * (g % 2):256 * (g % 2) + 256],
                                                k_stack[0:MROWS, s.au, g, tok], q_heads[0:MROWS, g, :, tok],
                                                start=True, stop=True)
                last.then_inc(pe_logit, 1)

            def weigh(s, j):
                need(pe, exp_done, 8 * s.ab + 2 * j + 2)
                if j == 0:
                    need(pe, vals_done, s.ab + 1)
                    need(pe, ml_done, s.ab + 1)
                else:
                    need(pe, otok_done, NT * s.ab + j)
                for m in range(H // 2):
                    last = nc.tensor.matmul(ps_at[:, VC * m:VC * (m + 1)], probs[:, j % 2, m, :, :].rearrange("p n q -> p (n q)"),
                                            vals[:, s.au, j, m, :], start=True, stop=True)
                last.then_inc(pe_pv, 1)

            def spread_gate(s, e):
                if e == 0:
                    need(pe, gate_done, s.ab + 1)
                    if s.finish:
                        need(pe, ln_sum[1], s.fb + 1)
                need(pe, gates_done, E * s.ab + e)
                tiles_t(ps_gate, lambda j: gate[:, s.au, e, j:j + 1].broadcast_to([P, P]), pe_gate)

            def step(s):
                if s.attend:
                    score(s, 0)
                    score(s, 1)
                if s.project:
                    need(pe, ld_xt[s.pu], 16 * s.ph + 16)
                    need(pe, vals_done, s.pb)
                    nc.tensor.matmul(ps_pf[:], wq[:], xt[:, s.pu, :], start=True, stop=True).then_inc(pe_q, 1)
                if s.finish:
                    need(pe, moe_done, s.fb + 1)
                    need(pe, gates_done, E * (min(s.ab, NB) if isinstance(s.t, int) else s.ab))
                    tiles_t(ps_gate, lambda j: moe_t[:, P * j:P * (j + 1)], pe_moet)
                if s.experts:
                    hidden(s, 0)
                for c in range(SLOTS):
                    if s.experts and c + 1 < NC:
                        hidden(s, c + 1)
                    if s.project and c == 1:
                        need(pe, ql_done, s.pb + 1)
                        nc.tensor.matmul(ps_pf[:], wk[:], xt[:, s.pu, :], start=True, stop=True).then_inc(pe_k, 1)
                    if s.attend:
                        for j in {0: (2, 3), 1: (4,), 2: (5, 6), 3: (7,)}.get(c, ()):
                            score(s, j)
                    if s.attend and c == 4:
                        need(pe, max_done, 8 * (s.ab + 1))
                        need(pe, x1l_done, s.ab)
                        for j in range(NT):
                            last = nc.tensor.transpose(ps_at[0:H, P * j:P * (j + 1)], smax[:, j, :], ident[:])
                        last.then_inc(pe_maxt, 1)
                    if s.finish and c == 5:
                        need(pe, ln_out[1], s.fb + 1)
                        if s.project:
                            need(pe, kl_done, s.pb + 1)
                        else:
                            need(pe, vals_done, NB)
                            need(pe, ln_sum[2], s.fb)
                        tiles_t(ps_pf, lambda j: x2[:, j, :], pe_x2t)
                    if s.finish and c == 7:
                        need(pe, x2t_done, s.fb + 1)
                        for j in range(NT):
                            last = nc.tensor.matmul(ps_pf[:, P * j:P * (j + 1)], x2_t[:, P * j:P * (j + 1)],
                                                    ffw[:], start=True, stop=True)
                        last.then_inc(pe_ffn, 1)
                    if s.attend and 6 <= c < 10:
                        logit(s, 2 * (c - 6))
                        logit(s, 2 * (c - 6) + 1)
                    if s.attend and 7 <= c < 11:
                        weigh(s, c - 7)
                    if s.project and c == 10:
                        need(pe, kl_done, s.pb + 1)
                        if s.finish:
                            need(pe, ln_sum[2], s.fb + 1)
                        for j in range(NT):
                            last = nc.tensor.matmul(ps_pf[:, P * j:P * (j + 1)], xt[:, s.pu, P * j:P * (j + 1)],
                                                    wv[:], start=True, stop=True)
                        last.then_inc(pe_v, 1)
                    if s.attend and c == 11:
                        need(pe, otok_done, NT * (s.ab + 1))
                        tiles_t(ps_at, lambda j: o_tok[:, j, :], pe_ot)
                    if s.attend and c == 12:
                        need(pe, ot_done, s.ab + 1)
                        for j in range(NT):
                            last = nc.tensor.matmul(ps_at[:, P * j:P * (j + 1)], o_t[:, P * j:P * (j + 1)],
                                                    wo[:], start=True, stop=True)
                        last.then_inc(pe_op, 1)
                    if s.attend:
                        for e in GATE_SLOTS.get(c, ()):
                            spread_gate(s, e)
                    if s.attend and c == 15:
                        need(pe, ln_out[0], s.ab + 1)
                        tiles_t(ps_at, lambda j: x1[:, s.au, j, :], pe_x1t)
                    if s.experts:
                        expert_out(s, c)

            pipeline(pe, step)


def build(nc, shapes, out_shape):
    args = [nc.dram_tensor(f"in_{name}", list(shape), dt, kind="ExternalInput").ap() for name, shape, dt in shapes]
    out = nc.dram_tensor("out_0", list(out_shape), F32, kind="ExternalOutput").ap()
    decoder_layer(nc, *args, out)


def kernel(x, ctx_512, itok_BxS2xS_0_7, L0_attn_Wq, L0_attn_bq, L0_attn_Wk, L0_attn_bk, L0_attn_Wv, L0_attn_bv,
           L0_attn_Wo, L0_attn_bo, L0_xattn_proj_in, L0_xattn_proj_out, L0_ffn_W, L0_ffn_b, L0_ffn_logits, L0_ffn_u):
    import concourse.bacc as bacc
    from concourse.bass_utils import run_bass_kernel_spmd

    def tiles(a):
        return np.ascontiguousarray(np.asarray(a).reshape(NB, NT, P, -1).transpose(0, 2, 1, 3))

    def con(a):
        return np.ascontiguousarray(a)

    x = np.asarray(x)
    slopes = np.power(np.float32(2.0), np.linspace(-4.0, -0.3, H, dtype=np.float32))
    decay = np.exp(-(np.arange(L, dtype=np.float64)[:, None] * slopes[None, :].astype(np.float64))).astype(np.float32)
    headmask = (np.arange(P)[:, None] % TERM // HD == np.arange(HG)[None, :]).astype(np.float32)
    arrays = {
        "x_tok": tiles(x.reshape(B * L, D)),
        "x_t": con(x.reshape(NB, BLK, D).transpose(0, 2, 1)),
        "gate_w": tiles(np.asarray(ctx_512).transpose(0, 2, 1).reshape(B * L, K)),
        "gate_e": tiles(np.asarray(itok_BxS2xS_0_7).transpose(0, 2, 1).reshape(B * L, K)),
        "wq_t": con(np.asarray(L0_attn_Wq).T), "bq": con(np.asarray(L0_attn_bq).reshape(D, 1)),
        "wk_t": con(np.asarray(L0_attn_Wk).T), "bk": con(np.asarray(L0_attn_bk).reshape(D, 1)),
        "wv_t": con(np.asarray(L0_attn_Wv).T), "bv": con(np.asarray(L0_attn_bv).reshape(D, 1)),
        "wo_t": con(np.asarray(L0_attn_Wo).T), "bo": con(np.asarray(L0_attn_bo).reshape(1, D)),
        "w_in": con(np.asarray(L0_xattn_proj_in).reshape(E * DH, D).T),
        "w_out": con(np.asarray(L0_xattn_proj_out).transpose(0, 2, 1).reshape(NC, P, D).transpose(1, 0, 2)),
        "ffn_w": con(np.asarray(L0_ffn_W).transpose(1, 0, 2)), "ffn_b": con(L0_ffn_b),
        "logits": con(np.asarray(L0_ffn_logits).reshape(1, NOPS)), "u": con(np.asarray(L0_ffn_u).reshape(1, NOPS)),
        "ident": np.eye(P, dtype=np.float32),
        "decay": con(np.concatenate([decay, decay])),
        "headmask": headmask,
        "iota": con(np.broadcast_to(np.arange(NOPS, dtype=np.float32), (P, NOPS))),
    }
    nc = bacc.Bacc("TRN2", target_bir_lowering=False, num_devices=1)
    build(nc, [(n, a.shape, mybir.dt.from_np(a.dtype)) for n, a in arrays.items()], (NB, P, NT, D))
    r = run_bass_kernel_spmd(nc, [{f"in_{n}": a for n, a in arrays.items()}], core_ids=[0])
    y = r.results[0]["out_0"]
    return con(y.transpose(0, 2, 1, 3)).reshape(B, L, D)
```

```python
from contextlib import ExitStack

import concourse.bass as bass
import numpy as np
from concourse import mybir

F32 = mybir.dt.float32
F32R = mybir.dt.float32r
F16 = mybir.dt.float16
BF16 = mybir.dt.bfloat16
I32 = mybir.dt.int32
ALU = mybir.AluOpType
ACT = mybir.ActivationFunctionType
AX = mybir.AxisListType

P = 128
B, L, D = 128, 64, 128
H, HD = 16, 8
E, DH = 8, 256
K = 64
NOPS = 8
BLK = 512
NB = B * L // BLK
NT = BLK // P
NC = E * DH // P
NG, HG = 4, 4
TERM = HG * HD
ROWS = 3 * TERM
MROWS = ROWS + 2
MAXSCALE = 256.0
VC = 2 * 2 * (HD + 1)
EPS = 1e-5
SCALE = float(1.0 / np.sqrt(HD))
SLOTS = NC
ROWSLEN = D + 2 * NOPS
FIRST = 2 * D + 2 + HG
REST = 3 * D + 1 + H + E + NOPS
HB, HP = 2, 4
GROWS = 3 * 32
ROWS_SLOT = 2
PICK_SLOTS = {0: (0,), 1: (1,), 2: (2,), 4: (3,), 5: (4,), 6: (5,), 7: (6,), 8: (7,)}
TREE_SLOTS = {9: (0,), 10: (1, 2), 11: (3,), 12: (4,)}
SPLIT_SLOT = 14
GATE_SLOTS = {3: (0,), 4: (1,), 5: (2,), 7: (3,), 9: (4,), 11: (5,), 12: (6,), 13: (7,)}
KHEAD_SLOTS = {c: (c - 1,) for c in range(1, 9)}
QHEAD_SLOTS = {5: (0, 1), 7: (2, 3), 10: (4,), 11: (5,), 12: (6,), 13: (7,)}
SCORE_SLOTS = {9: (0,), 10: (1,), 11: (2,), 12: (3,), 13: (4,), 14: (5, 6), 15: (7,)}
MAX_SLOTS = {10: (0,), 11: (1,), 12: (2,), 13: (3,), 14: (4, 5), 15: (6, 7)}
LOGIT_SLOTS = {2: (0, 1), 4: (2, 3), 6: (4, 5), 8: (6, 7)}
WEIGH_SLOTS = {3: 0, 5: 1, 7: 2, 9: 3}
NORM_SLOTS = {4: 0, 6: 1, 8: 2, 10: 3}
FIRST_KHEADS = 3
K_SLOT, Q_SLOT, V_SLOT = 9, 11, 3


class Step:

    def __init__(self, t, i, u):
        self.t, self.i, self.u = t, i, u
        fixed = isinstance(t, int)
        self.queries = not fixed or 0 <= t + 3 < NB
        self.project = not fixed or 0 <= t + 2 < NB
        self.attend = not fixed or 0 <= t + 1 < NB
        self.experts = not fixed or 0 <= t < NB
        self.finish = not fixed or 0 <= t - 1 < NB
        self.qb, self.qu, self.qh = t + 3, 1 - u, i + 1 + u
        self.pb, self.pu, self.ph = t + 2, u, i + 1
        self.ab, self.au, self.ah = t + 1, 1 - u, i + u
        self.eb, self.eu = t, u
        self.fb, self.fu, self.fh = t - 1, 1 - u, i - 1 + u


def pipeline(eng, run, after_first=None, after_second=None):
    for t in range(-3, 3):
        run(Step(t, t // 2, t % 2))
        if t == -3 and after_first:
            after_first()
        if t == -2 and after_second:
            after_second()
    with eng.Fori(1, NB // 2 - 2) as i:
        run(Step(2 * i + 1, i, 1))
        run(Step(2 * i + 2, i + 1, 0))
    for t in range(NB - 3, NB + 1):
        run(Step(t, t // 2, t % 2))


def due(count):
    return not isinstance(count, int) or count > 0


def decoder_layer(nc, x_tok, x_t, gate_w, gate_e, first_c, rest_c, rows_c, w_in, w_out, ffn_w, ffn_b, out):
    ctx = ExitStack()
    with ctx:
        def sb(name, shape, dt=F32):
            return ctx.enter_context(nc.sbuf_tensor(name, shape, dt))

        def sem(name):
            return ctx.enter_context(nc.semaphore(name))

        first = sb("first", [P, FIRST])
        rest = sb("rest", [P, REST])
        rows = sb("rows", [P, ROWSLEN])
        wk, wq = first[:, 0:D], first[:, D:2 * D]
        bks, bqs = first[:, 2 * D:2 * D + 1], first[:, 2 * D + 1:2 * D + 2]
        headmask = first[:, 2 * D + 2:2 * D + 2 + HG]
        ident, wv, wo = (rest[:, D * n:D * (n + 1)] for n in range(3))
        small = 3 * D
        bvs = rest[:, small:small + 1]
        decay = rest[:, small + 1:small + 1 + H]
        expertmask = rest[:, small + 1 + H:small + 1 + H + E]
        iota = rest[:, small + 1 + H + E:REST]
        attn_bias = rows[:, 0:D]
        choice_in = rows[:, D:D + 2 * NOPS].rearrange("p (n o) -> p n o", o=NOPS)
        ident_b = sb("ident_b", [P, P], BF16)
        select = sb("select", [P, E, P], BF16)
        win_h = sb("win_h", [P, NC * P], F32R)
        win_l = sb("win_l", [P, NC * P], F32R)
        wout_h = sb("wout_h", [P, NC * D], F32R)
        wout_l = sb("wout_l", [P, NC * D], F32R)
        ffw = sb("ffw", [P, D])
        ffb = sb("ffb", [P, D])
        xt = sb("xt", [P, 2, BLK])
        xtok = sb("xtok", [P, 2, NT, D])
        gw = sb("gw", [P, 2, NT, K])
        ge = sb("ge", [P, 2, NT, K], I32)
        qh = sb("qh", [P, BLK], F16)
        ql = sb("ql", [P, BLK], F16)
        kh = sb("kh", [P, BLK], F16)
        kl = sb("kl", [P, BLK], F16)
        q_stack = sb("q_stack", [P, 2, NG, BLK], F16)
        k_stack = sb("k_stack", [P, 2, NG, BLK], F16)
        k_heads = sb("k_heads", [P, NG, HG, BLK], F16)
        q_heads = sb("q_heads", [P, NG, HG, BLK], F16)
        smax = sb("smax", [P, NT, H])
        mh = sb("mh", [H, BLK], F16)
        ml = sb("ml", [H, BLK], F16)
        probs = sb("probs", [P, 2, H // 2, 2, L])
        vals = sb("vals", [P, 2, NT, H // 2, VC])
        rden = sb("rden", [P, H // 2, 4])
        o_tok = sb("o_tok", [P, NT, D])
        o_t = sb("o_t", [P, BLK])
        picked = sb("picked", [P, E, NT, K])
        gate = sb("gate", [P, NT, E])
        gate_rest = sb("gate_rest", [P, NT, E])
        gate_parts = sb("gate_parts", [P, NT, 3, 32], BF16)
        gate_rows = sb("gate_rows", [P, BLK], BF16)
        gates = sb("gates", [P, 2, E, BLK])
        x1 = sb("x1", [P, 2, NT, D])
        x1h = sb("x1h", [P, 2, BLK], F32R)
        x1l = sb("x1l", [P, 2, BLK], F32R)
        hid = sb("hid", [P, HB, BLK])
        hid_h = sb("hid_h", [P, HP, BLK], F32R)
        hid_l = sb("hid_l", [P, HB, BLK], F32R)
        x2b = sb("x2b", [P, NT, D])
        turned = sb("turned", [P, BLK])
        ln_x = sb("ln_x", [P, 3, NT, D])
        ln_st = sb("ln_st", [P, 3, NT, 6])
        ln_mv = sb("ln_mv", [P, 3, NT, 2])
        ln_ve = sb("ln_ve", [P, 3, NT])
        ln_rs = sb("ln_rs", [P, 3, NT])
        ln_shift = sb("ln_shift", [P, 3, NT])
        minus_half = sb("minus_half", [P, NT])
        choice = sb("choice", [P, 12, NOPS])
        pick = sb("pick", [P, 8])

        def bank(name, cols=512):
            return ctx.enter_context(nc.psum_tensor(name, [P, cols], F32))

        ps_hid = [bank("ps_hid0"), bank("ps_hid1")]
        ps_moe = bank("ps_moe")
        ps_score = [bank("ps_score0"), bank("ps_score1")]
        ps_pf = bank("ps_pf")
        ps_at = bank("ps_at")
        ps_gate = bank("ps_gate")

        s_first, s_rest, s_rows, s_ffw = sem("s_first"), sem("s_rest"), sem("s_rows"), sem("s_ffw")
        s_raw = [sem(f"s_raw{n}") for n in range(4)]
        s_set = sem("s_set")
        s_seta = sem("s_seta")
        s_setp = sem("s_setp")
        s_sett = sem("s_sett")
        ld_xt = [sem("ld_xt0"), sem("ld_xt1")]
        ld_xtok = [sem("ld_xtok0"), sem("ld_xtok1")]
        ld_gate = [sem("ld_gate0"), sem("ld_gate1")]
        pe_q, pe_k, pe_v = sem("pe_q"), sem("pe_k"), sem("pe_v")
        qh_done, ql_done, kh_done, kl_done = sem("qh_done"), sem("ql_done"), sem("kh_done"), sem("kl_done")
        vals_done = sem("vals_done")
        kstack_in, qstack_in = sem("kstack_in"), sem("qstack_in")
        first_kheads = sem("first_kheads")
        kheads_done, qheads_done = sem("kheads_done"), sem("qheads_done")
        pe_score = sem("pe_score")
        max_done = sem("max_done")
        pe_maxt = sem("pe_maxt")
        mh_done, ml_done = sem("mh_done"), sem("ml_done")
        max_in = sem("max_in")
        pe_logit = sem("pe_logit")
        exp_done = sem("exp_done")
        pe_pv = sem("pe_pv")
        rden_done = sem("rden_done")
        otok_done = sem("otok_done")
        pe_ot, ot_done, pe_op = sem("pe_ot"), sem("ot_done"), sem("pe_op")
        xb_done = sem("xb_done")
        eq_done = sem("eq_done")
        picked_done = sem("picked_done")
        tree_done = sem("tree_done")
        rest_done = sem("rest_done")
        gate_done = sem("gate_done")
        pe_rows, rows_done = sem("pe_rows"), sem("rows_done")
        pe_gate = sem("pe_gate")
        gates_done = sem("gates_done")
        ln_sum = [sem(f"ln_sum{n}") for n in range(3)]
        ln_stat = [sem(f"ln_stat{n}") for n in range(3)]
        ln_var = [sem(f"ln_var{n}") for n in range(3)]
        ln_eps = [sem(f"ln_eps{n}") for n in range(3)]
        ln_rstd = [sem(f"ln_rstd{n}") for n in range(3)]
        ln_shifted = [sem(f"ln_shifted{n}") for n in range(3)]
        ln_out = [sem(f"ln_out{n}") for n in range(3)]
        pe_x1t, x1h_done, x1l_done = sem("pe_x1t"), sem("x1h_done"), sem("x1l_done")
        pe_hid, hid_done, pe_moe = sem("pe_hid"), sem("hid_done"), sem("pe_moe")
        high_done = sem("high_done")
        low_even, low_odd = sem("low_even"), sem("low_odd")
        moe_done, pe_moet = sem("moe_done"), sem("pe_moet")
        pe_x2t, x2t_done, x2b_done, pe_ffn = sem("pe_x2t"), sem("x2t_done"), sem("x2b_done"), sem("pe_ffn")
        stored = sem("stored")

        WH = NC * P // 2
        ffw_all = gates[:, 0, :, 0:D]
        ffb_all = gates[:, 1, :, 0:D]
        w_raw = gates[:, :, :, D:2 * D]
        x2, y = ln_x[:, 1, :, :], ln_x[:, 2, :, :]
        vals_v = vals[:].rearrange("p u j m (h b x) -> p u j b h m x", h=2, b=2)

        block = ctx.enter_context(nc.Block())

        @block.sync
        def _(sp):
            sp.dma_start(first[:], first_c).then_inc(s_first, 16)
            sp.dma_start(xt[:, 0, :], x_t[0]).then_inc(ld_xt[0], 16)
            sp.dma_start(gw[:, 0, :, :], gate_w[0]).then_inc(ld_gate[0], 16)
            sp.dma_start(ge[:, 0, :, :], gate_e[0]).then_inc(ld_gate[0], 16)
            sp.dma_start(xt[:, 1, :], x_t[1]).then_inc(ld_xt[1], 16)
            sp.dma_start(rest[:], rest_c).then_inc(s_rest, 16)

            def more_setup():
                for n in range(2):
                    sp.dma_start(w_raw[:, n, :, :], w_in[:, WH * n:WH * (n + 1)].rearrange("p (c d) -> p c d", d=D)).then_inc(s_raw[n], 16)
                sp.dma_start(gw[:, 1, :, :], gate_w[1]).then_inc(ld_gate[1], 16)
                sp.dma_start(ge[:, 1, :, :], gate_e[1]).then_inc(ld_gate[1], 16)
                sp.dma_start(rows[:], rows_c.broadcast_to([P, ROWSLEN])).then_inc(s_rows, 16)
                for b in range(2):
                    sp.dma_start(xtok[:, b, :, :], x_tok[b]).then_inc(ld_xtok[b], 16)
                sp.dma_start(ffw_all, ffn_w).then_inc(s_ffw, 16)
                sp.dma_start(ffb_all, ffn_b.broadcast_to([P, NOPS, D])).then_inc(s_ffw, 16)

            def load_w_out():
                for n in range(2):
                    sp.wait_ge(s_set, n + 1)
                    sp.dma_start(w_raw[:, n, :, :], w_out[:, WH * n:WH * (n + 1)].rearrange("p (c d) -> p c d", d=D)).then_inc(s_raw[2 + n], 16)

            def step(s):
                if s.attend:
                    sp.wait_ge(ml_done, s.ab + 1)
                    for n, src in enumerate((mh, ml)):
                        sp.dma_start(q_heads[ROWS + n:ROWS + n + 1, :, :, :].rearrange("o g h c -> o (g h) c"),
                                     src[:, :]).then_inc(max_in, 16)
                fixed = isinstance(s.t, int)
                if not fixed or 2 <= s.t + 3 < NB:
                    sp.wait_ge(pe_v, s.pb)
                    sp.dma_start(xt[:, s.au, :], x_t[s.t + 3]).then_inc(ld_xt[s.au], 16)
                    sp.wait_ge(picked_done, E * s.pb)
                    sp.dma_start(gw[:, s.au, :, :], gate_w[s.t + 3]).then_inc(ld_gate[s.au], 16)
                    sp.dma_start(ge[:, s.au, :, :], gate_e[s.t + 3]).then_inc(ld_gate[s.au], 16)
                if not fixed or 2 <= s.t + 2 < NB:
                    sp.wait_ge(ln_sum[0], s.ab)
                    sp.dma_start(xtok[:, s.u, :, :], x_tok[s.t + 2]).then_inc(ld_xtok[s.u], 16)
                if s.queries:
                    sp.wait_ge(kl_done, s.qb + 1)
                    for n, src in enumerate((kh, kh, kl)):
                        for g in range(NG):
                            sp.dma_start(k_stack[TERM * n:TERM * (n + 1), s.qu, g, :],
                                         src[TERM * g:TERM * (g + 1), :]).then_inc(kstack_in, 16)
                if s.queries:
                    sp.wait_ge(ql_done, s.qb + 1)
                    for n, src in enumerate((qh, ql, qh)):
                        for g in range(NG):
                            sp.dma_start(q_stack[TERM * n:TERM * (n + 1), s.qu, g, :],
                                         src[TERM * g:TERM * (g + 1), :]).then_inc(qstack_in, 16)
                if s.finish:
                    sp.wait_ge(ln_out[2], s.fb + 1)
                    sp.dma_start(out[s.fb], y).then_inc(stored, 16)

            pipeline(sp, step, more_setup, load_w_out)
            sp.wait_ge(stored, 16 * NB)

        @block.gpsimd
        def _(pool):
            nc.gpsimd.memset(minus_half[:], -0.5).then_inc(s_setp, 1)
            nc.gpsimd.memset(vals[:], 0.0).then_inc(s_setp, 1)
            nc.gpsimd.memset(gate_parts[:], 0.0).then_inc(s_setp, 1)
            pool.wait_ge(s_setp, 3)

            def rstd(n, b):
                pool.wait_ge(ln_eps[n], b + 1)
                nc.gpsimd.tensor_tensor(ln_rs[:, n, :], ln_ve[:, n, :], minus_half[:], ALU.pow).then_inc(ln_rstd[n], 1)

            def pick_expert(s, e):
                nc.gpsimd.tensor_scalar(picked[:, e, :, :], ge[:, s.pu, :, :], float(e), None, ALU.is_equal).then_inc(eq_done, 1)
                pool.wait_ge(eq_done, E * s.pb + e + 1)
                nc.gpsimd.tensor_tensor(picked[:, e, :, :], picked[:, e, :, :], gw[:, s.pu, :, :], ALU.mult).then_inc(picked_done, 1)

            def sum_gates(s, n):
                if n == 0:
                    pool.wait_ge(picked_done, E * (s.pb + 1))
                else:
                    pool.wait_ge(tree_done, 5 * s.pb + n)
                pk = picked[:].rearrange("p e j k -> p (e j) k")
                w = K // 2 >> n
                nc.gpsimd.tensor_tensor(pk[:, :, 0:w], pk[:, :, 0:w], pk[:, :, w:2 * w], ALU.add).then_inc(tree_done, 1)

            def split_gates(s):
                pk = picked[:].rearrange("p e j k -> p (e j) k")
                pool.wait_ge(tree_done, 5 * s.pb + 5)
                first, second = (pk[:, :, n:n + 1].rearrange("p (e j) o -> p e j o", e=E) for n in range(2))
                by_e = "p j e -> p e j"
                parts = [gate_parts[:, :, n, 0:E] for n in range(3)]
                if due(s.pb):
                    pool.wait_ge(pe_rows, s.pb)
                nc.gpsimd.tensor_tensor(parts[0].rearrange(by_e).unsqueeze(3), first, second, ALU.add).then_inc(rest_done, 1)
                nc.gpsimd.tensor_tensor(gate[:].rearrange(by_e).unsqueeze(3), first, second, ALU.add).then_inc(rest_done, 1)
                pool.wait_ge(rest_done, 4 * s.pb + 2)
                nc.gpsimd.tensor_tensor(parts[1], gate[:], parts[0], ALU.subtract).then_inc(rest_done, 1)
                nc.gpsimd.tensor_tensor(gate_rest[:], gate[:], parts[0], ALU.subtract).then_inc(rest_done, 1)
                pool.wait_ge(rest_done, 4 * s.pb + 4)
                nc.gpsimd.tensor_tensor(parts[2], gate_rest[:], parts[1], ALU.subtract).then_inc(gate_done, 1)

            def low_part(s, c):
                pool.wait_ge(high_done, NC * s.eb + c + 1)
                if due(NC * s.eb + c + 1 - HB):
                    pool.wait_ge(pe_moe, NC * s.eb + c + 1 - HB)
                nc.gpsimd.tensor_tensor(hid_l[:, c % HB, :], hid[:, c % HB, :], hid_h[:, c % HP, :].bitcast(F32),
                                        ALU.subtract).then_inc(low_odd, 1)

            def step(s):
                if s.project:
                    if due(s.pb):
                        pool.wait_ge(gate_done, s.pb)
                    pool.wait_ge(ld_gate[s.pu], 32 * s.ph + 32)
                if s.attend:
                    if isinstance(s.t, int) and s.t == -1:
                        pool.wait_ge(s_set, 6)
                    pool.wait_ge(ld_xtok[s.au], 16 * s.ah + 16)
                    nc.gpsimd.tensor_tensor(xtok[:, s.au, :, :], xtok[:, s.au, :, :],
                                            attn_bias.unsqueeze(1).broadcast_to([P, NT, D]), ALU.add).then_inc(xb_done, 1)
                for c in range(SLOTS):
                    if s.finish and c == 3:
                        rstd(1, s.fb)
                    if s.finish and c == 4:
                        pool.wait_ge(ln_out[1], s.fb + 1)
                        if due(s.fb):
                            pool.wait_ge(ln_sum[2], s.fb)
                        nc.gpsimd.tensor_tensor(x2b[:], x2, ffb[:].unsqueeze(1).broadcast_to([P, NT, D]),
                                                ALU.add).then_inc(x2b_done, 1)
                    if s.project:
                        for e in PICK_SLOTS.get(c, ()):
                            pick_expert(s, e)
                        for n in TREE_SLOTS.get(c, ()):
                            sum_gates(s, n)
                        if c == SPLIT_SLOT:
                            split_gates(s)
                    if s.finish and c == 10:
                        rstd(2, s.fb)
                    if s.attend and c == 13:
                        rstd(0, s.ab)
                    if s.experts and c % 2 == 1:
                        low_part(s, c)

            pipeline(pool, step)

        @block.scalar
        def _(act):
            act.wait_ge(s_first, 16)

            def setup():
                for n, dst in enumerate((win_h, win_h, wout_h, wout_h)):
                    act.wait_ge(s_raw[n], 16)
                    nc.scalar.activation(dst[:, WH * (n % 2):WH * (n % 2 + 1)].rearrange("p (c d) -> p c d", d=D),
                                         w_raw[:, n % 2, :, :], ACT.Copy).then_inc(s_seta, 1)
                act.wait_ge(s_set, 8)
                nc.scalar.activation(choice[:, 3, :], choice[:, 2, :], ACT.Exp, accum_out=pick[:, 1:2]).then_inc(s_seta, 1)
                act.wait_ge(s_seta, 5)
                nc.scalar.activation(pick[:, 2:3], pick[:, 1:2], ACT.Ln).then_inc(s_seta, 1)
                nc.scalar.activation(choice[:, 4, :], choice_in[:, 1, :], ACT.Ln).then_inc(s_seta, 1)
                act.wait_ge(s_seta, 7)
                nc.scalar.activation(choice[:, 5, :], choice[:, 4, :], ACT.Ln, scale=-1.0).then_inc(s_seta, 1)

            def high(psum, dst, bias, full, free, b, done):
                act.wait_ge(full, b + 1)
                if due(192 * b):
                    act.wait_ge(free, 192 * b)
                nc.scalar.activation(dst[:], psum[:], ACT.Identity, bias=bias[:, 0:1]).then_inc(done, 1)

            def keep_gate(s, e):
                act.wait_ge(pe_gate, E * s.ab + e + 1)
                if e == 0:
                    if due(NC * (s.ab - 1)):
                        act.wait_ge(hid_done, NC * (s.ab - 1))
                nc.scalar.activation(gates[:, s.au, e, :], ps_gate[:], ACT.Copy).then_inc(gates_done, 1)

            def keep_rows(s):
                act.wait_ge(pe_rows, s.ab + 1)
                if due(E * s.ab):
                    act.wait_ge(pe_gate, E * s.ab)
                nc.scalar.activation(gate_rows[0:GROWS, :], ps_gate[0:GROWS, :], ACT.Copy).then_inc(rows_done, 1)

            def exps(s, j):
                act.wait_ge(pe_logit, 8 * s.ab + j + 1)
                if j % 2 == 0:
                    if due(NT * s.ab + j // 2 - 1):
                        act.wait_ge(pe_pv, NT * s.ab + j // 2 - 1)
                nc.scalar.activation(probs[:, j // 2 % 2, :, j % 2, :], ps_score[j % 2][:].rearrange("p (m q) -> p m q", q=L),
                                     ACT.Exp, scale=SCALE).then_inc(exp_done, 1)

            def scale_out(n, b, dst):
                act.wait_ge(ln_shifted[n], b + 1)
                for j in range(NT):
                    last = nc.scalar.activation(dst[:, j, :], ln_x[:, n, j, :], ACT.Identity,
                                                bias=ln_shift[:, n, j:j + 1], scale=ln_rs[:, n, j:j + 1])
                last.then_inc(ln_out[n], 1)

            def k_head(s, n):
                h, g = n // 2, slice(2 * (n % 2), 2 * (n % 2) + 2)
                if n == 0:
                    act.wait_ge(kstack_in, 192 * (s.pb + 1))
                    if due(8 * s.pb):
                        act.wait_ge(pe_score, 8 * s.pb)
                ins = nc.scalar.activation(k_heads[0:ROWS, g, h, :], k_stack[0:ROWS, s.pu, g, :], ACT.Copy,
                                           scale=headmask[0:ROWS, h:h + 1])
                if n == 2 * HG - 1 or isinstance(s.t, int) and s.t == -2 and n == FIRST_KHEADS - 1:
                    ins.then_inc(kheads_done, 1)

            def step(s):
                if s.finish:
                    act.wait_ge(pe_moe, NC * (s.fb + 1))
                    if due(s.fb):
                        act.wait_ge(pe_ffn, s.fb)
                    nc.scalar.activation(turned[:], ps_moe[:], ACT.Copy).then_inc(moe_done, 1)
                if s.attend:
                    act.wait_ge(pe_maxt, s.ab + 1)
                    if due(32 * s.ab):
                        act.wait_ge(max_in, 32 * s.ab)
                    nc.scalar.activation(mh[:], ps_at[0:H, :], ACT.Copy, scale=1.0 / MAXSCALE).then_inc(mh_done, 1)
                for c in range(SLOTS):
                    if s.experts:
                        act.wait_ge(hid_done, NC * s.eb + c + 1)
                        if due(NC * s.eb + c + 1 - HP):
                            act.wait_ge(pe_moe, NC * s.eb + c + 1 - HP)
                        nc.scalar.activation(hid_h[:, c % HP, :], hid[:, c % HB, :], ACT.Copy).then_inc(high_done, 1)
                    if s.attend and c == ROWS_SLOT:
                        keep_rows(s)
                    if s.queries and c == Q_SLOT:
                        high(ps_pf, qh, bqs, pe_q, qstack_in, s.qb, qh_done)
                    if s.queries and c == K_SLOT:
                        high(ps_pf, kh, bks, pe_k, kstack_in, s.qb, kh_done)
                    if s.finish and c == 4:
                        scale_out(1, s.fb, x2)
                    if s.finish and c == 5:
                        act.wait_ge(pe_x2t, s.fb + 1)
                        act.wait_ge(pe_moet, s.fb + 1)
                        nc.scalar.activation(turned[:], ps_pf[:], ACT.Copy).then_inc(x2t_done, 1)
                    if s.attend:
                        for j in LOGIT_SLOTS.get(c, ()):
                            exps(s, j)
                    if s.attend and c == 11:
                        act.wait_ge(pe_ot, s.ab + 1)
                        if due(s.ab):
                            act.wait_ge(pe_op, s.ab)
                        nc.scalar.activation(o_t[:], ps_at[:], ACT.Copy).then_inc(ot_done, 1)
                    if s.finish and c == 12:
                        scale_out(2, s.fb, y)
                    if s.attend and c == 14:
                        scale_out(0, s.ab, x1[:, s.au, :, :])
                    if s.attend:
                        for e in GATE_SLOTS.get(c, ()):
                            keep_gate(s, e)
                    if s.project:
                        for n in KHEAD_SLOTS.get(c, ()):
                            if not (isinstance(s.t, int) and s.t == -2 and n >= FIRST_KHEADS):
                                k_head(s, n)
                    if s.attend and c == 15:
                        act.wait_ge(pe_x1t, s.ab + 1)
                        nc.scalar.activation(x1h[:, s.au, :], ps_at[:], ACT.Copy).then_inc(x1h_done, 1)

            pipeline(act, step, after_second=setup)

        @block.vector
        def _(dve):
            nc.vector.memset(k_stack[ROWS:MROWS, :, :, :], -MAXSCALE)
            dve.wait_ge(s_first, 16)
            dec = decay.rearrange("p (h m) -> p h m", h=2)
            count = [0]

            def did(ins):
                count[0] += 1
                ins.then_inc(s_set, 1)
                dve.wait_ge(s_set, count[0])

            def need_rest():
                dve.wait_ge(s_rest, 16)
                dve.wait_ge(s_setp, 3)

            def setup():
                nc.vector.memset(pick[:], 0.0)
                for n, (low_part, high_part) in enumerate(((win_l, win_h), (win_l, win_h), (wout_l, wout_h), (wout_l, wout_h))):
                    half = slice(WH * (n % 2), WH * (n % 2 + 1))
                    dve.wait_ge(s_seta, n + 1)
                    did(nc.vector.tensor_tensor(low_part[:, half].rearrange("p (c d) -> p c d", d=D), w_raw[:, n % 2, :, :],
                                                high_part[:, half].rearrange("p (c d) -> p c d", d=D).bitcast(F32), ALU.subtract))
                    if n == 1:
                        for par in range(2):
                            for j in range(NT):
                                for b in range(2):
                                    r = slice(L * b, L * b + L)
                                    nc.vector.tensor_copy(vals_v[r, par, j, b, :, :, HD], dec[r])
                        nc.vector.tensor_copy(ident_b[:], ident)
                        did(nc.vector.tensor_copy(select[:], expertmask.unsqueeze(2).broadcast_to([P, E, P])))
                dve.wait_ge(s_rows, 16)
                dve.wait_ge(s_sett, 1)
                did(nc.vector.tensor_tensor(attn_bias, ps_at[:, 0:D], attn_bias, ALU.add))
                did(nc.vector.tensor_reduce(pick[:, 0:1], choice_in[:, 0, :], AX.X, ALU.max))
                did(nc.vector.tensor_scalar(choice[:, 2, :], choice_in[:, 0, :], pick[:, 0:1], None, ALU.subtract))
                dve.wait_ge(s_seta, 8)
                did(nc.vector.tensor_scalar(choice[:, 6, :], choice[:, 2, :], pick[:, 2:3], None, ALU.subtract))
                did(nc.vector.tensor_tensor(choice[:, 7, :], choice[:, 6, :], choice[:, 5, :], ALU.subtract))
                did(nc.vector.tensor_reduce(pick[:, 3:4], choice[:, 7, :], AX.X, ALU.max))
                did(nc.vector.tensor_scalar(choice[:, 8, :], choice[:, 7, :], pick[:, 3:4], float(NOPS), ALU.is_lt, ALU.mult))
                did(nc.vector.tensor_tensor(choice[:, 9, :], choice[:, 8, :], iota, ALU.add))
                did(nc.vector.tensor_reduce(pick[:, 4:5], choice[:, 9, :], AX.X, ALU.min))
                did(nc.vector.tensor_scalar(choice[:, 10, :], iota, pick[:, 4:5], None, ALU.is_equal))
                dve.wait_ge(s_ffw, 32)
                for n in range(NOPS):
                    for dst, src in ((ffw, ffw_all), (ffb, ffb_all)):
                        if n == 0:
                            did(nc.vector.tensor_scalar(dst[:], src[:, 0, :], choice[:, 10, 0:1], None, ALU.mult))
                        else:
                            did(nc.vector.scalar_tensor_tensor(out=dst[:], in0=src[:, n, :], scalar=choice[:, 10, n:n + 1],
                                                               in1=dst[:], op0=ALU.mult, op1=ALU.add))

            def low(psum, dst, high, bias, ready, b, done):
                dve.wait_ge(ready, b + 1)
                nc.vector.scalar_tensor_tensor(out=dst[:], in0=psum[:], scalar=bias[:, 0:1], in1=high[:],
                                               op0=ALU.add, op1=ALU.subtract).then_inc(done, 1)

            def keep_vals(s):
                dve.wait_ge(pe_v, s.pb + 1)
                if due(NT * (s.pb - 1)):
                    dve.wait_ge(pe_pv, NT * (s.pb - 1))
                for j in range(NT):
                    v = ps_pf[:, P * j:P * (j + 1)].rearrange("p (h m x) -> p h m x", h=2, x=HD)
                    for b in range(2):
                        r = slice(L * b, L * b + L)
                        last = nc.vector.tensor_tensor(vals_v[r, s.pu, j, b, :, :, 0:HD], v[r],
                                                       dec[r].unsqueeze(3).broadcast_to([L, 2, H // 2, HD]), ALU.mult)
                last.then_inc(vals_done, 1)

            def maximum(b, j):
                dve.wait_ge(pe_score, 8 * b + j + 1)
                if j == 0:
                    if due(b):
                        dve.wait_ge(pe_maxt, b)
                nc.vector.tensor_reduce(smax[:, j // 2, 8 * (j % 2):8 * (j % 2) + 8],
                                        ps_score[j % 2][:].rearrange("p (h k) -> p h k", k=L), AX.X,
                                        ALU.max).then_inc(max_done, 1)

            def normalise(s, j):
                dve.wait_ge(pe_pv, NT * s.ab + j + 1)
                acc = ps_at[:, 0:H // 2 * VC].rearrange("p (m q x) -> p m q x", q=4, x=HD + 1)
                nc.vector.reciprocal(rden[:], acc[:, :, :, HD]).then_inc(rden_done, 1)
                if j == 0:
                    if due(s.ab):
                        dve.wait_ge(pe_ot, s.ab)
                dve.wait_ge(rden_done, NT * s.ab + j + 1)
                for h2 in range(2):
                    for b in range(2):
                        q = 2 * h2 + b
                        r = slice(L * h2, L * h2 + L)
                        dst = o_tok[L * b:L * b + L, j, 64 * h2:64 * h2 + 64].rearrange("p (m x) -> p m x", x=HD)
                        last = nc.vector.tensor_tensor(dst, acc[r, :, q, 0:HD],
                                                       rden[r, :, q].unsqueeze(2).broadcast_to([L, H // 2, HD]), ALU.mult)
                last.then_inc(otok_done, 1)

            def first_k_heads(s):
                dve.wait_ge(kstack_in, 192)
                for n in range(FIRST_KHEADS, 2 * HG):
                    h, g = n // 2, slice(2 * (n % 2), 2 * (n % 2) + 2)
                    last = nc.vector.tensor_scalar(k_heads[0:ROWS, g, h, :], k_stack[0:ROWS, s.pu, g, :],
                                                   headmask[0:ROWS, h:h + 1], None, ALU.mult)
                last.then_inc(first_kheads, 1)

            def q_head(s, n):
                h, pair = n % HG, n // HG
                if n == 0:
                    dve.wait_ge(qstack_in, 192 * (s.pb + 1))
                if h == 0:
                    if due(8 * s.ab + 4 * pair + 4):
                        dve.wait_ge(pe_logit, 8 * s.ab + 4 * pair + 4)
                tok = slice(2 * P * pair, 2 * P * pair + 2 * P)
                ins = nc.vector.tensor_scalar(q_heads[0:ROWS, :, h, tok], q_stack[0:ROWS, s.pu, :, tok],
                                              headmask[0:ROWS, h:h + 1], None, ALU.mult)
                if n == 2 * HG - 1:
                    ins.then_inc(qheads_done, 1)

            def stats(n, b):
                dve.wait_ge(ln_sum[n], b + 1)
                for j in range(NT):
                    last = nc.vector.bn_stats(ln_st[:, n, j, :], ln_x[:, n, j, :])
                last.then_inc(ln_stat[n], 1)

            def variance(n, b):
                for j in range(NT):
                    last = nc.vector.bn_aggr(ln_mv[:, n, j, :], ln_st[:, n, j, :])
                last.then_inc(ln_var[n], 1)

            def add_eps(n, b):
                dve.wait_ge(ln_var[n], b + 1)
                nc.vector.tensor_scalar(ln_ve[:, n, :], ln_mv[:, n, :, 1], EPS, None, ALU.add).then_inc(ln_eps[n], 1)

            def shift(n, b):
                dve.wait_ge(ln_rstd[n], b + 1)
                nc.vector.scalar_tensor_tensor(out=ln_shift[:, n, :], in0=ln_mv[:, n, :, 0], scalar=-1.0, in1=ln_rs[:, n, :],
                                               op0=ALU.mult, op1=ALU.mult).then_inc(ln_shifted[n], 1)

            def step(s):
                for c in range(SLOTS):
                    if s.finish and c == 2:
                        dve.wait_ge(ln_stat[1], s.fb + 1)
                    if s.finish and c == 10:
                        dve.wait_ge(ln_stat[2], s.fb + 1)
                    if s.attend and c == 13:
                        dve.wait_ge(ln_stat[0], s.ab + 1)
                    if s.experts:
                        dve.wait_ge(pe_hid, NC * s.eb + c + 1)
                        if c % 2 == 0:
                            dve.wait_ge(gates_done, E * s.eb + c // 2 + 1)
                        if due(NC // 2 * s.eb + c // 2):
                            dve.wait_ge(low_odd if c % 2 else low_even, NC // 2 * s.eb + c // 2)
                        nc.vector.scalar_tensor_tensor(out=hid[:, c % HB, :], in0=ps_hid[c % 2][:], scalar=0.0,
                                                       in1=gates[:, s.eu, c // 2, :], op0=ALU.max,
                                                       op1=ALU.mult).then_inc(hid_done, 1)
                    if s.finish and c == 2:
                        variance(1, s.fb)
                        add_eps(1, s.fb)
                    if s.finish and c == 10:
                        variance(2, s.fb)
                        add_eps(2, s.fb)
                    if s.attend and c == 13:
                        variance(0, s.ab)
                        add_eps(0, s.ab)
                    if s.experts and c % 2 == 1:
                        dve.wait_ge(high_done, NC * s.eb + c)
                        if due(NC * s.eb + c - HB):
                            dve.wait_ge(pe_moe, NC * s.eb + c - HB)
                        nc.vector.tensor_tensor(hid_l[:, (c - 1) % HB, :], hid[:, (c - 1) % HB, :],
                                                hid_h[:, (c - 1) % HP, :].bitcast(F32), ALU.subtract).then_inc(low_even, 1)
                    if s.attend and c == 0:
                        dve.wait_ge(mh_done, s.ab + 1)
                        nc.vector.scalar_tensor_tensor(out=ml[:], in0=ps_at[0:H, :], scalar=1.0 / MAXSCALE, in1=mh[:],
                                                       op0=ALU.mult, op1=ALU.subtract).then_inc(ml_done, 1)
                    if s.finish and c == 0:
                        dve.wait_ge(pe_moet, s.fb + 1)
                        nc.vector.tensor_tensor(ln_x[:, 1, :, :], ps_gate[:].rearrange("p (j d) -> p j d", d=D),
                                                x1[:, s.fu, :, :], ALU.add).then_inc(ln_sum[1], 1)
                    if s.finish and c == 1:
                        stats(1, s.fb)
                    if isinstance(s.t, int) and s.t == -2 and c == V_SLOT:
                        first_k_heads(s)
                    if s.project and c == V_SLOT:
                        keep_vals(s)
                    if s.finish and c == 3:
                        shift(1, s.fb)
                    if s.attend and c in NORM_SLOTS:
                        normalise(s, NORM_SLOTS[c])
                    if s.finish and c == 8:
                        dve.wait_ge(pe_ffn, s.fb + 1)
                        if due(16 * s.fb):
                            dve.wait_ge(stored, 16 * s.fb)
                        dve.wait_ge(x2b_done, s.fb + 1)
                        nc.vector.tensor_tensor(ln_x[:, 2, :, :], ps_pf[:].rearrange("p (j d) -> p j d", d=D),
                                                x2b[:], ALU.add).then_inc(ln_sum[2], 1)
                    if s.finish and c == 9:
                        stats(2, s.fb)
                    if s.queries and c == Q_SLOT + 1:
                        low(ps_pf, ql, qh, bqs, qh_done, s.qb, ql_done)
                    if s.queries and c == K_SLOT + 1:
                        low(ps_pf, kl, kh, bks, kh_done, s.qb, kl_done)
                    if s.project:
                        for n in QHEAD_SLOTS.get(c, ()):
                            q_head(s, n)
                        for j in MAX_SLOTS.get(c, ()):
                            maximum(s.pb, j)
                    if s.finish and c == 11:
                        shift(2, s.fb)
                    if s.attend and c == 12:
                        dve.wait_ge(pe_op, s.ab + 1)
                        dve.wait_ge(xb_done, s.ab + 1)
                        nc.vector.tensor_tensor(ln_x[:, 0, :, :], ps_at[:].rearrange("p (j d) -> p j d", d=D),
                                                xtok[:, s.au, :, :], ALU.add).then_inc(ln_sum[0], 1)
                        stats(0, s.ab)
                    if s.attend and c == 14:
                        shift(0, s.ab)
                    if s.attend and c == 15:
                        dve.wait_ge(x1h_done, s.ab + 1)
                        nc.vector.tensor_tensor(x1l[:, s.au, :], ps_at[:], x1h[:, s.au, :].bitcast(F32),
                                                ALU.subtract).then_inc(x1l_done, 1)

            pipeline(dve, step, need_rest, setup)

        @block.tensor
        def _(pe):
            pe.wait_ge(s_first, 16)

            def need_rest():
                pe.wait_ge(s_rest, 16)

            def setup():
                nc.tensor.matmul(ps_at[:, 0:D], bvs[:, 0:1].broadcast_to([P, P]), wo, start=True, stop=True).then_inc(s_sett, 1)
                pe.wait_ge(s_set, 6)

            def hidden(s, c):
                if c == 0:
                    pe.wait_ge(x1h_done, s.eb + 1)
                    pe.wait_ge(x1l_done, s.eb + 1)
                if due(NC * s.eb + c - 1):
                    pe.wait_ge(hid_done, NC * s.eb + c - 1)
                w = slice(P * c, P * (c + 1))
                nc.tensor.matmul(ps_hid[c % 2][:], win_h[:, w], x1h[:, s.eu, :], start=True, stop=False)
                nc.tensor.matmul(ps_hid[c % 2][:], win_l[:, w], x1h[:, s.eu, :], start=False, stop=False)
                nc.tensor.matmul(ps_hid[c % 2][:], win_h[:, w], x1l[:, s.eu, :], start=False, stop=True).then_inc(pe_hid, 1)

            def expert_out(b, c):
                pe.wait_ge(high_done, NC * b + c + 1)
                if c == 0:
                    if due(b):
                        pe.wait_ge(moe_done, b)
                w = slice(D * c, D * (c + 1))
                nc.tensor.matmul(ps_moe[:], wout_h[:, w], hid_h[:, c % HP, :], start=(c == 0), stop=False)
                nc.tensor.matmul(ps_moe[:], wout_l[:, w], hid_h[:, c % HP, :], start=False, stop=False)
                pe.wait_ge(low_odd if c % 2 else low_even, NC // 2 * b + c // 2 + 1)
                nc.tensor.matmul(ps_moe[:], wout_h[:, w], hid_l[:, c % HB, :], start=False,
                                 stop=(c == NC - 1)).then_inc(pe_moe, 1)

            def tiles_t(dst, src, done):
                for j in range(NT):
                    last = nc.tensor.transpose(dst[:, P * j:P * (j + 1)], src(j), ident)
                last.then_inc(done, 1)

            def score(b, par, j):
                if j == 0:
                    pe.wait_ge(kheads_done, b + 1)
                    if isinstance(b, int) and b == 0:
                        pe.wait_ge(first_kheads, 1)
                    pe.wait_ge(qstack_in, 192 * (b + 1))
                if j < 2:
                    if due(8 * b - 1 + j):
                        pe.wait_ge(exp_done, 8 * b - 1 + j)
                else:
                    pe.wait_ge(max_done, 8 * b + j - 1)
                for g in (2 * (j % 2), 2 * (j % 2) + 1):
                    for h in range(2):
                        tok = slice(P * (j // 2) + L * h, P * (j // 2) + L * h + L)
                        last = nc.tensor.matmul(ps_score[j % 2][L * h:L * h + L, 256 * (g % 2):256 * (g % 2) + 256],
                                                q_stack[0:ROWS, par, g, tok], k_heads[0:ROWS, g, :, tok],
                                                start=True, stop=True)
                last.then_inc(pe_score, 1)

            def logit(s, j):
                if j == 0:
                    pe.wait_ge(max_in, 32 * (s.ab + 1))
                    pe.wait_ge(qheads_done, s.ab + 1)
                if j < 2:
                    pe.wait_ge(max_done, 8 * s.ab + 7 + j)
                else:
                    pe.wait_ge(exp_done, 8 * s.ab + j - 1)
                for g in (2 * (j % 2), 2 * (j % 2) + 1):
                    for b in range(2):
                        tok = slice(P * (j // 2) + L * b, P * (j // 2) + L * b + L)
                        last = nc.tensor.matmul(ps_score[j % 2][L * b:L * b + L, 256 * (g % 2):256 * (g % 2) + 256],
                                                k_stack[0:MROWS, s.au, g, tok], q_heads[0:MROWS, g, :, tok],
                                                start=True, stop=True)
                last.then_inc(pe_logit, 1)

            def weigh(s, j):
                pe.wait_ge(exp_done, 8 * s.ab + 2 * j + 2)
                if j == 0:
                    pe.wait_ge(vals_done, s.ab + 1)
                    pe.wait_ge(ml_done, s.ab + 1)
                else:
                    pe.wait_ge(otok_done, NT * s.ab + j)
                for m in range(H // 2):
                    last = nc.tensor.matmul(ps_at[:, VC * m:VC * (m + 1)], probs[:, j % 2, m, :, :].rearrange("p n q -> p (n q)"),
                                            vals[:, s.au, j, m, :], start=True, stop=True)
                last.then_inc(pe_pv, 1)

            def gate_to_rows(s):
                pe.wait_ge(gate_done, s.ab + 1)
                if s.finish:
                    pe.wait_ge(ln_sum[1], s.fb + 1)
                if due(E * s.ab):
                    pe.wait_ge(gates_done, E * s.ab)
                for j in range(NT):
                    last = nc.tensor.matmul(ps_gate[0:GROWS, P * j:P * (j + 1)],
                                            gate_parts[:, j, :, :].rearrange("p n e -> p (n e)"), ident_b[:], start=True, stop=True)
                last.then_inc(pe_rows, 1)

            def spread_gate(s, e):
                if e == 0:
                    pe.wait_ge(rows_done, s.ab + 1)
                if due(E * s.ab + e):
                    pe.wait_ge(gates_done, E * s.ab + e)
                nc.tensor.matmul(ps_gate[:], select[0:GROWS, e, :], gate_rows[0:GROWS, :], start=True, stop=True).then_inc(pe_gate, 1)

            def step(s):
                if s.finish:
                    expert_out(s.fb, NC - 1)
                if s.attend:
                    pe.wait_ge(max_done, 8 * (s.ab + 1))
                    if due(s.ab):
                        pe.wait_ge(x1l_done, s.ab)
                    for j in range(NT):
                        last = nc.tensor.transpose(ps_at[0:H, P * j:P * (j + 1)], smax[:, j, :], ident)
                    last.then_inc(pe_maxt, 1)
                if s.experts:
                    hidden(s, 0)
                for c in range(SLOTS):
                    if s.experts and c + 1 < NC:
                        hidden(s, c + 1)
                    if s.finish and c == 0:
                        pe.wait_ge(moe_done, s.fb + 1)
                        pe.wait_ge(gates_done, E * (min(s.ab, NB) if isinstance(s.t, int) else s.ab))
                        tiles_t(ps_gate, lambda j: turned[:, P * j:P * (j + 1)], pe_moet)
                    if s.queries and c == K_SLOT:
                        pe.wait_ge(ld_xt[s.qu], 16 * s.qh + 16)
                        if s.project:
                            pe.wait_ge(vals_done, s.pb + 1)
                        if due(s.fb + 1):
                            pe.wait_ge(ln_sum[2], s.fb + 1)
                        nc.tensor.matmul(ps_pf[:], wk, xt[:, s.qu, :], start=True, stop=True).then_inc(pe_k, 1)
                    if s.queries and c == Q_SLOT:
                        pe.wait_ge(kl_done, s.qb + 1)
                        nc.tensor.matmul(ps_pf[:], wq, xt[:, s.qu, :], start=True, stop=True).then_inc(pe_q, 1)
                    if s.project and c == V_SLOT:
                        pe.wait_ge(ql_done, s.pb + 1)
                        for j in range(NT):
                            last = nc.tensor.matmul(ps_pf[:, P * j:P * (j + 1)], xt[:, s.pu, P * j:P * (j + 1)],
                                                    wv, start=True, stop=True)
                        last.then_inc(pe_v, 1)
                    if s.finish and c == 5:
                        pe.wait_ge(ln_out[1], s.fb + 1)
                        if s.project:
                            pe.wait_ge(vals_done, s.pb + 1)
                        else:
                            pe.wait_ge(vals_done, NB)
                            pe.wait_ge(ln_sum[2], s.fb)
                        tiles_t(ps_pf, lambda j: x2[:, j, :], pe_x2t)
                    if s.finish and c == 7:
                        pe.wait_ge(x2t_done, s.fb + 1)
                        for j in range(NT):
                            last = nc.tensor.matmul(ps_pf[:, P * j:P * (j + 1)], turned[:, P * j:P * (j + 1)],
                                                    ffw[:], start=True, stop=True)
                        last.then_inc(pe_ffn, 1)
                    if s.attend:
                        for j in LOGIT_SLOTS.get(c, ()):
                            logit(s, j)
                    if s.attend and c in WEIGH_SLOTS:
                        weigh(s, WEIGH_SLOTS[c])
                    if s.attend and c == 11:
                        pe.wait_ge(otok_done, NT * (s.ab + 1))
                        tiles_t(ps_at, lambda j: o_tok[:, j, :], pe_ot)
                    if s.attend and c == 12:
                        pe.wait_ge(ot_done, s.ab + 1)
                        for j in range(NT):
                            last = nc.tensor.matmul(ps_at[:, P * j:P * (j + 1)], o_t[:, P * j:P * (j + 1)],
                                                    wo, start=True, stop=True)
                        last.then_inc(pe_op, 1)
                    if s.attend and c == ROWS_SLOT:
                        gate_to_rows(s)
                    if s.attend:
                        for e in GATE_SLOTS.get(c, ()):
                            spread_gate(s, e)
                    if s.project:
                        for j in SCORE_SLOTS.get(c, ()):
                            score(s.pb, s.pu, j)
                    if s.attend and c == 15:
                        pe.wait_ge(ln_out[0], s.ab + 1)
                        tiles_t(ps_at, lambda j: x1[:, s.au, j, :], pe_x1t)
                    if s.experts and c > 0:
                        expert_out(s.eb, c - 1)

            pipeline(pe, step, need_rest, setup)


def build(nc, shapes, out_shape):
    args = [nc.dram_tensor(f"in_{name}", list(shape), dt, kind="ExternalInput").ap() for name, shape, dt in shapes]
    out = nc.dram_tensor("out_0", list(out_shape), F32, kind="ExternalOutput").ap()
    decoder_layer(nc, *args, out)


def kernel(x, ctx_512, itok_BxS2xS_0_7, L0_attn_Wq, L0_attn_bq, L0_attn_Wk, L0_attn_bk, L0_attn_Wv, L0_attn_bv,
           L0_attn_Wo, L0_attn_bo, L0_xattn_proj_in, L0_xattn_proj_out, L0_ffn_W, L0_ffn_b, L0_ffn_logits, L0_ffn_u):
    import concourse.bacc as bacc
    from concourse.bass_utils import run_bass_kernel_spmd

    def tiles(a):
        return np.ascontiguousarray(np.asarray(a).reshape(NB, NT, P, -1).transpose(0, 2, 1, 3))

    def con(a):
        return np.ascontiguousarray(a)

    x = np.asarray(x)
    slopes = np.power(np.float32(2.0), np.linspace(-4.0, -0.3, H, dtype=np.float32))
    decay = np.exp(-(np.arange(L, dtype=np.float64)[:, None] * slopes[None, :].astype(np.float64))).astype(np.float32)
    headmask = (np.arange(P)[:, None] % TERM // HD == np.arange(HG)[None, :]).astype(np.float32)
    expertmask = (np.arange(P)[:, None] % 32 == np.arange(E)[None, :]).astype(np.float32)
    arrays = {
        "x_tok": tiles(x.reshape(B * L, D)),
        "x_t": con(x.reshape(NB, BLK, D).transpose(0, 2, 1)),
        "gate_w": tiles(np.asarray(ctx_512).transpose(0, 2, 1).reshape(B * L, K)),
        "gate_e": tiles(np.asarray(itok_BxS2xS_0_7).transpose(0, 2, 1).reshape(B * L, K)),
        "first": con(np.concatenate([np.asarray(L0_attn_Wk).T, np.asarray(L0_attn_Wq).T, np.asarray(L0_attn_bk).reshape(D, 1),
                                     np.asarray(L0_attn_bq).reshape(D, 1), headmask], axis=1)),
        "rest": con(np.concatenate([np.eye(P, dtype=np.float32), np.asarray(L0_attn_Wv).T, np.asarray(L0_attn_Wo).T,
                                    np.asarray(L0_attn_bv).reshape(D, 1), np.concatenate([decay, decay]), expertmask,
                                    np.broadcast_to(np.arange(NOPS, dtype=np.float32), (P, NOPS))], axis=1)),
        "rows": con(np.concatenate([np.asarray(a).reshape(1, -1) for a in
                                    (L0_attn_bo, L0_ffn_logits, L0_ffn_u)], axis=1)),
        "w_in": con(np.asarray(L0_xattn_proj_in).reshape(E * DH, D).T),
        "w_out": con(np.asarray(L0_xattn_proj_out).transpose(0, 2, 1).reshape(NC, P, D).transpose(1, 0, 2).reshape(P, NC * D)),
        "ffn_w": con(np.asarray(L0_ffn_W).transpose(1, 0, 2)), "ffn_b": con(np.asarray(L0_ffn_b).reshape(1, NOPS, D)),
    }
    nc = bacc.Bacc("TRN2", target_bir_lowering=False, num_devices=1)
    build(nc, [(n, a.shape, mybir.dt.from_np(a.dtype)) for n, a in arrays.items()], (NB, P, NT, D))
    r = run_bass_kernel_spmd(nc, [{f"in_{n}": a for n, a in arrays.items()}], core_ids=[0])
    y = r.results[0]["out_0"]
    return con(y.transpose(0, 2, 1, 3)).reshape(B, L, D)
```

```python
from contextlib import ExitStack

import concourse.bass as bass
import numpy as np
from concourse import mybir

F32 = mybir.dt.float32
F32R = mybir.dt.float32r
F16 = mybir.dt.float16
BF16 = mybir.dt.bfloat16
I32 = mybir.dt.int32
ALU = mybir.AluOpType
ACT = mybir.ActivationFunctionType
AX = mybir.AxisListType

P = 128
B, L, D = 128, 64, 128
H, HD = 16, 8
E, DH = 8, 256
K = 64
NOPS = 8
BLK = 512
NB = B * L // BLK
NT = BLK // P
NC = E * DH // P
NG, HG = 4, 4
TERM = HG * HD
ROWS = 3 * TERM
MROWS = ROWS + 2
MAXSCALE = 256.0
VC = 2 * 2 * (HD + 1)
EPS = 1e-5
SCALE = float(1.0 / np.sqrt(HD))
SLOTS = NC
ROWSLEN = D + 2 * NOPS
FIRST = 2 * D + 2 + HG
REST = 3 * D + 1 + H + E + NOPS
HB, HP = 2, 4
GROWS = 3 * 32
ROWS_SLOT = 1
PICK_SLOTS = {1: (0, 1), 2: (2,), 4: (3, 4), 6: (5, 6), 8: (7,)}
TREE_SLOTS = {8: (0,), 11: (1,), 12: (2, 3), 14: (4,)}
SPLIT_SLOT = 14
GATE_SLOTS = {2: (0,), 4: (1,), 6: (2,), 8: (3,), 11: (4,), 12: (5,), 13: (6,), 14: (7,)}
KHEAD_SLOTS = {1: (0,), 2: (1, 2), 5: (3, 4), 6: (5,), 7: (6, 7)}
QHEAD_SLOTS = {5: (0,), 6: (1,), 7: (2,), 8: (3, 4), 9: (5,), 10: (6, 7)}
SCORE_SLOTS = {9: (0,), 10: (1,), 11: (2,), 13: (3, 4), 14: (5,), 15: (6, 7)}
MAX_SLOTS = {10: (0,), 11: (1,), 12: (2,), 13: (3,), 14: (4, 5, 6), 15: (7,)}
LOGIT_SLOTS = {2: (0, 1), 4: (2, 3), 6: (4, 5), 8: (6, 7)}
FIRST_LOGIT_SLOTS = {2: (0, 1), 3: (2, 3), 5: (4, 5), 7: (6, 7)}
WEIGH_SLOTS = {3: 0, 6: 1, 7: 2, 9: 3}
NORM_SLOTS = {4: 0, 6: 1, 8: 2, 10: 3}
SETUP_B = 6
FIRST_KHEADS = 3
K_SLOT, Q_SLOT, V_SLOT = 9, 11, 3
KL_SLOT, QL_SLOT = 9, 12
X2_SLOT, X2T_SLOT, FFN_SLOT, SUM_SLOT, STAT_SLOT, SHIFT_SLOT, Y_SLOT = 3, 5, 7, 7, 8, 12, 12
RSTD1_SLOT, X2B_SLOT, RSTD2_SLOT, RSTD0_SLOT = 3, 4, 11, 12
VAR1_SLOT, SHIFT1_SLOT, SHIFT0_SLOT, X1_SLOT = 2, 3, 14, 14
EO_FIRST = (3, 5, 10, 13)
HIGH_LAST = (4, 10, 13)
LOW_LAST = (5,)
POOL_FIRST = (1, 3, 11, 13)
OT_SLOT, WO_SLOT = 11, 12


class Step:

    def __init__(self, t, i, u):
        self.t, self.i, self.u = t, i, u
        fixed = isinstance(t, int)
        self.fixed = t if fixed else None
        self.queries = not fixed or 0 <= t + 3 < NB
        self.project = not fixed or 0 <= t + 2 < NB
        self.attend = not fixed or 0 <= t + 1 < NB
        self.experts = not fixed or 0 <= t < NB
        self.finish = not fixed or 0 <= t - 1 < NB
        self.qb, self.qu, self.qh = t + 3, 1 - u, i + 1 + u
        self.pb, self.pu, self.ph = t + 2, u, i + 1
        self.ab, self.au, self.ah = t + 1, 1 - u, i + u
        self.eb, self.eu = t, u
        self.fb, self.fu, self.fh = t - 1, 1 - u, i - 1 + u


def pipeline(eng, run, after_first=None, after_second=None):
    for t in range(-3, 3):
        run(Step(t, t // 2, t % 2))
        if t == -3 and after_first:
            after_first()
        if t == -2 and after_second:
            after_second()
    with eng.Fori(1, NB // 2 - 2) as i:
        run(Step(2 * i + 1, i, 1))
        run(Step(2 * i + 2, i + 1, 0))
    for t in range(NB - 3, NB + 1):
        run(Step(t, t // 2, t % 2))


def due(count):
    return not isinstance(count, int) or count > 0


def decoder_layer(nc, x_tok, x_t, gate_w, gate_e, first_c, rest_c, rows_c, w_in, w_out, ffn_w, ffn_b, out):
    ctx = ExitStack()
    with ctx:
        def sb(name, shape, dt=F32):
            return ctx.enter_context(nc.sbuf_tensor(name, shape, dt))

        def sem(name):
            return ctx.enter_context(nc.semaphore(name))

        first = sb("first", [P, FIRST])
        rest = sb("rest", [P, REST])
        rows = sb("rows", [P, ROWSLEN])
        wk, wq = first[:, 0:D], first[:, D:2 * D]
        bks, bqs = first[:, 2 * D:2 * D + 1], first[:, 2 * D + 1:2 * D + 2]
        headmask = first[:, 2 * D + 2:2 * D + 2 + HG]
        ident, wv, wo = (rest[:, D * n:D * (n + 1)] for n in range(3))
        small = 3 * D
        bvs = rest[:, small:small + 1]
        decay = rest[:, small + 1:small + 1 + H]
        expertmask = rest[:, small + 1 + H:small + 1 + H + E]
        iota = rest[:, small + 1 + H + E:REST]
        attn_bias = rows[:, 0:D]
        choice_in = rows[:, D:D + 2 * NOPS].rearrange("p (n o) -> p n o", o=NOPS)
        ident_b = sb("ident_b", [P, P], BF16)
        select = sb("select", [P, E, P], BF16)
        win_h = sb("win_h", [P, NC * P], F32R)
        win_l = sb("win_l", [P, NC * P], F32R)
        wout_h = sb("wout_h", [P, NC * D], F32R)
        wout_l = sb("wout_l", [P, NC * D], F32R)
        ffw = sb("ffw", [P, D])
        ffb = sb("ffb", [P, D])
        xt = sb("xt", [P, 2, BLK])
        xtok = sb("xtok", [P, 2, NT, D])
        gw = sb("gw", [P, 2, NT, K])
        ge = sb("ge", [P, 2, NT, K], I32)
        qh = sb("qh", [P, BLK], F16)
        ql = sb("ql", [P, BLK], F16)
        kh = sb("kh", [P, BLK], F16)
        kl = sb("kl", [P, BLK], F16)
        q_stack = sb("q_stack", [P, 2, NG, BLK], F16)
        k_stack = sb("k_stack", [P, 2, NG, BLK], F16)
        k_heads = sb("k_heads", [P, NG, HG, BLK], F16)
        q_heads = sb("q_heads", [P, NG, HG, BLK], F16)
        smax = sb("smax", [P, NT, H])
        mh = sb("mh", [H, BLK], F16)
        ml = sb("ml", [H, BLK], F16)
        probs = sb("probs", [P, 2, H // 2, 2, L])
        vals = sb("vals", [P, 2, NT, H // 2, VC])
        rden = sb("rden", [P, H // 2, 4])
        o_tok = sb("o_tok", [P, NT, D])
        o_t = sb("o_t", [P, BLK])
        picked = sb("picked", [P, E, NT, K])
        gate = sb("gate", [P, NT, E])
        gate_rest = sb("gate_rest", [P, NT, E])
        gate_parts = sb("gate_parts", [P, NT, 3, 32], BF16)
        gate_rows = sb("gate_rows", [P, BLK], BF16)
        gates = sb("gates", [P, 2, E, BLK])
        x1 = sb("x1", [P, 2, NT, D])
        x1h = sb("x1h", [P, 2, BLK], F32R)
        x1l = sb("x1l", [P, 2, BLK], F32R)
        hid = sb("hid", [P, HB, BLK])
        hid_h = sb("hid_h", [P, HP, BLK], F32R)
        hid_l = sb("hid_l", [P, HB, BLK], F32R)
        x2b = sb("x2b", [P, NT, D])
        turned = sb("turned", [P, BLK])
        ln_x = sb("ln_x", [P, 3, NT, D])
        ln_st = sb("ln_st", [P, 3, NT, 6])
        ln_mv = sb("ln_mv", [P, 3, NT, 2])
        ln_ve = sb("ln_ve", [P, 3, NT])
        ln_rs = sb("ln_rs", [P, 3, NT])
        ln_shift = sb("ln_shift", [P, 3, NT])
        minus_half = sb("minus_half", [P, NT])
        choice = sb("choice", [P, 12, NOPS])
        pick = sb("pick", [P, 8])

        def bank(name, cols=512):
            return ctx.enter_context(nc.psum_tensor(name, [P, cols], F32))

        ps_hid = [bank("ps_hid0"), bank("ps_hid1")]
        ps_moe = bank("ps_moe")
        ps_score = [bank("ps_score0"), bank("ps_score1")]
        ps_pf = bank("ps_pf")
        ps_at = bank("ps_at")
        ps_gate = bank("ps_gate")

        s_first, s_rest, s_rows, s_ffw = sem("s_first"), sem("s_rest"), sem("s_rows"), sem("s_ffw")
        s_raw = [sem(f"s_raw{n}") for n in range(4)]
        s_set = sem("s_set")
        s_seta = sem("s_seta")
        s_setp = sem("s_setp")
        s_sett = sem("s_sett")
        ld_xt = [sem("ld_xt0"), sem("ld_xt1")]
        ld_xtok = [sem("ld_xtok0"), sem("ld_xtok1")]
        ld_gate = [sem("ld_gate0"), sem("ld_gate1")]
        pe_q, pe_k, pe_v = sem("pe_q"), sem("pe_k"), sem("pe_v")
        qh_done, ql_done, kh_done, kl_done = sem("qh_done"), sem("ql_done"), sem("kh_done"), sem("kl_done")
        vals_done = sem("vals_done")
        kstack_in, qstack_in = sem("kstack_in"), sem("qstack_in")
        first_kheads = sem("first_kheads")
        kheads_done, qheads_done = sem("kheads_done"), sem("qheads_done")
        pe_score = sem("pe_score")
        max_done = sem("max_done")
        pe_maxt = sem("pe_maxt")
        mh_done, ml_done = sem("mh_done"), sem("ml_done")
        max_in = sem("max_in")
        pe_logit = sem("pe_logit")
        exp_done = sem("exp_done")
        pe_pv = sem("pe_pv")
        rden_done = sem("rden_done")
        otok_done = sem("otok_done")
        pe_ot, ot_done, pe_op = sem("pe_ot"), sem("ot_done"), sem("pe_op")
        xb_done = sem("xb_done")
        eq_done = sem("eq_done")
        picked_done = sem("picked_done")
        tree_done = sem("tree_done")
        rest_done = sem("rest_done")
        gate_done = sem("gate_done")
        pe_rows, rows_done = sem("pe_rows"), sem("rows_done")
        pe_gate = sem("pe_gate")
        gates_done = sem("gates_done")
        ln_sum = [sem(f"ln_sum{n}") for n in range(3)]
        ln_stat = [sem(f"ln_stat{n}") for n in range(3)]
        ln_var = [sem(f"ln_var{n}") for n in range(3)]
        ln_eps = [sem(f"ln_eps{n}") for n in range(3)]
        ln_rstd = [sem(f"ln_rstd{n}") for n in range(3)]
        ln_shifted = [sem(f"ln_shifted{n}") for n in range(3)]
        ln_out = [sem(f"ln_out{n}") for n in range(3)]
        pe_x1t, x1h_done, x1l_done = sem("pe_x1t"), sem("x1h_done"), sem("x1l_done")
        pe_hid, hid_done, pe_moe = sem("pe_hid"), sem("hid_done"), sem("pe_moe")
        high_done = sem("high_done")
        low_even, low_odd = sem("low_even"), sem("low_odd")
        moe_done, pe_moet = sem("moe_done"), sem("pe_moet")
        pe_x2t, x2t_done, x2b_done, pe_ffn = sem("pe_x2t"), sem("x2t_done"), sem("x2b_done"), sem("pe_ffn")
        stored = sem("stored")

        WH = NC * P // 2
        w_raw = gates[:, 1, :, 0:2 * D].rearrange("p c (n d) -> p n c d", n=2)
        ffw_all = gates[:, 1, :, 2 * D:3 * D]
        ffb_all = gates[:, 1, :, 3 * D:4 * D]
        x2, y = ln_x[:, 1, :, :], ln_x[:, 2, :, :]
        vals_v = vals[:].rearrange("p u j m (h b x) -> p u j b h m x", h=2, b=2)

        block = ctx.enter_context(nc.Block())

        @block.sync
        def _(sp):
            sp.dma_start(first[:], first_c).then_inc(s_first, 16)
            sp.dma_start(xt[:, 0, :], x_t[0]).then_inc(ld_xt[0], 16)
            sp.dma_start(gw[:, 0, :, :], gate_w[0]).then_inc(ld_gate[0], 16)
            sp.dma_start(ge[:, 0, :, :], gate_e[0]).then_inc(ld_gate[0], 16)
            sp.dma_start(xt[:, 1, :], x_t[1]).then_inc(ld_xt[1], 16)
            sp.dma_start(rest[:], rest_c).then_inc(s_rest, 16)

            def more_setup():
                for n in range(2):
                    sp.dma_start(w_raw[:, n, :, :], w_in[:, WH * n:WH * (n + 1)].rearrange("p (c d) -> p c d", d=D)).then_inc(s_raw[n], 16)
                sp.dma_start(gw[:, 1, :, :], gate_w[1]).then_inc(ld_gate[1], 16)
                sp.dma_start(ge[:, 1, :, :], gate_e[1]).then_inc(ld_gate[1], 16)
                sp.dma_start(rows[:], rows_c.broadcast_to([P, ROWSLEN])).then_inc(s_rows, 16)
                for b in range(2):
                    sp.dma_start(xtok[:, b, :, :], x_tok[b]).then_inc(ld_xtok[b], 16)
                sp.dma_start(ffw_all, ffn_w).then_inc(s_ffw, 16)
                sp.dma_start(ffb_all, ffn_b.broadcast_to([P, NOPS, D])).then_inc(s_ffw, 16)

            def load_w_out():
                for n in range(2):
                    sp.wait_ge(s_set, n + 1)
                    sp.dma_start(w_raw[:, n, :, :], w_out[:, WH * n:WH * (n + 1)].rearrange("p (c d) -> p c d", d=D)).then_inc(s_raw[2 + n], 16)

            def stack_q(b, par):
                sp.wait_ge(ql_done, b + 1)
                for n, src in enumerate((qh, ql, qh)):
                    for g in range(NG):
                        sp.dma_start(q_stack[TERM * n:TERM * (n + 1), par, g, :],
                                     src[TERM * g:TERM * (g + 1), :]).then_inc(qstack_in, 16)

            def step(s):
                if s.attend:
                    sp.wait_ge(ml_done, s.ab + 1)
                    for n, src in enumerate((mh, ml)):
                        sp.dma_start(q_heads[ROWS + n:ROWS + n + 1, :, :, :].rearrange("o g h c -> o (g h) c"),
                                     src[:, :]).then_inc(max_in, 16)
                if s.fixed == -1:
                    load_w_out()
                    stack_q(s.ab + 1, s.u)
                fixed = isinstance(s.t, int)
                if not fixed or 2 <= s.t + 3 < NB:
                    sp.wait_ge(pe_v, s.pb)
                    sp.dma_start(xt[:, s.au, :], x_t[s.t + 3]).then_inc(ld_xt[s.au], 16)
                    sp.wait_ge(picked_done, E * s.pb)
                    sp.dma_start(gw[:, s.au, :, :], gate_w[s.t + 3]).then_inc(ld_gate[s.au], 16)
                    sp.dma_start(ge[:, s.au, :, :], gate_e[s.t + 3]).then_inc(ld_gate[s.au], 16)
                if not fixed or 2 <= s.t + 2 < NB:
                    sp.wait_ge(ln_sum[0], s.ab)
                    sp.dma_start(xtok[:, s.u, :, :], x_tok[s.t + 2]).then_inc(ld_xtok[s.u], 16)
                if s.queries:
                    sp.wait_ge(kl_done, s.qb + 1)
                    for n, src in enumerate((kh, kh, kl)):
                        for g in range(NG):
                            sp.dma_start(k_stack[TERM * n:TERM * (n + 1), s.qu, g, :],
                                         src[TERM * g:TERM * (g + 1), :]).then_inc(kstack_in, 16)
                if s.queries and s.fixed != -2:
                    stack_q(s.qb, s.qu)
                if s.finish:
                    sp.wait_ge(ln_out[2], s.fb + 1)
                    sp.dma_start(out[s.fb], y).then_inc(stored, 16)

            pipeline(sp, step, more_setup)
            sp.wait_ge(stored, 16 * NB)

        @block.gpsimd
        def _(pool):
            nc.gpsimd.memset(minus_half[:], -0.5).then_inc(s_setp, 1)
            nc.gpsimd.memset(vals[:], 0.0).then_inc(s_setp, 1)
            nc.gpsimd.memset(gate_parts[:], 0.0).then_inc(s_setp, 1)
            pool.wait_ge(s_setp, 3)

            def rstd(n, b):
                pool.wait_ge(ln_eps[n], b + 1)
                nc.gpsimd.tensor_tensor(ln_rs[:, n, :], ln_ve[:, n, :], minus_half[:], ALU.pow).then_inc(ln_rstd[n], 1)

            def pick_expert(s, e):
                nc.gpsimd.tensor_scalar(picked[:, e, :, :], ge[:, s.pu, :, :], float(e), None, ALU.is_equal).then_inc(eq_done, 1)
                pool.wait_ge(eq_done, E * s.pb + e + 1)
                nc.gpsimd.tensor_tensor(picked[:, e, :, :], picked[:, e, :, :], gw[:, s.pu, :, :], ALU.mult).then_inc(picked_done, 1)

            def sum_gates(s, n):
                if n == 0:
                    pool.wait_ge(picked_done, E * (s.pb + 1))
                else:
                    pool.wait_ge(tree_done, 5 * s.pb + n)
                pk = picked[:].rearrange("p e j k -> p (e j) k")
                w = K // 2 >> n
                nc.gpsimd.tensor_tensor(pk[:, :, 0:w], pk[:, :, 0:w], pk[:, :, w:2 * w], ALU.add).then_inc(tree_done, 1)

            def split_gates(s):
                pk = picked[:].rearrange("p e j k -> p (e j) k")
                pool.wait_ge(tree_done, 5 * s.pb + 5)
                first, second = (pk[:, :, n:n + 1].rearrange("p (e j) o -> p e j o", e=E) for n in range(2))
                by_e = "p j e -> p e j"
                parts = [gate_parts[:, :, n, 0:E] for n in range(3)]
                if due(s.pb):
                    pool.wait_ge(pe_rows, s.pb)
                nc.gpsimd.tensor_tensor(parts[0].rearrange(by_e).unsqueeze(3), first, second, ALU.add).then_inc(rest_done, 1)
                nc.gpsimd.tensor_tensor(gate[:].rearrange(by_e).unsqueeze(3), first, second, ALU.add).then_inc(rest_done, 1)
                pool.wait_ge(rest_done, 4 * s.pb + 2)
                nc.gpsimd.tensor_tensor(parts[1], gate[:], parts[0], ALU.subtract).then_inc(rest_done, 1)
                nc.gpsimd.tensor_tensor(gate_rest[:], gate[:], parts[0], ALU.subtract).then_inc(rest_done, 1)
                pool.wait_ge(rest_done, 4 * s.pb + 4)
                nc.gpsimd.tensor_tensor(parts[2], gate_rest[:], parts[1], ALU.subtract).then_inc(gate_done, 1)

            def low_part(s, c):
                pool.wait_ge(high_done, NC * s.eb + c + 1)
                if due(NC * s.eb + c + 1 - HB):
                    pool.wait_ge(pe_moe, NC * s.eb + c + 1 - HB)
                nc.gpsimd.tensor_tensor(hid_l[:, c % HB, :], hid[:, c % HB, :], hid_h[:, c % HP, :].bitcast(F32),
                                        ALU.subtract).then_inc(low_odd, 1)

            def step(s):
                if s.project:
                    if due(s.pb):
                        pool.wait_ge(gate_done, s.pb)
                    pool.wait_ge(ld_gate[s.pu], 32 * s.ph + 32)
                if s.attend:
                    if s.fixed == -1:
                        pool.wait_ge(s_set, 6)
                    pool.wait_ge(ld_xtok[s.au], 16 * s.ah + 16)
                    nc.gpsimd.tensor_tensor(xtok[:, s.au, :, :], xtok[:, s.au, :, :],
                                            attn_bias.unsqueeze(1).broadcast_to([P, NT, D]), ALU.add).then_inc(xb_done, 1)
                for c in range(SLOTS):
                    if s.experts and c % 2 == 0 and c > 0 and c - 1 in POOL_FIRST:
                        low_part(s, c - 1)
                    if s.finish and c == RSTD1_SLOT:
                        rstd(1, s.fb)
                    if s.finish and c == X2B_SLOT:
                        pool.wait_ge(ln_out[1], s.fb + 1)
                        if due(s.fb):
                            pool.wait_ge(ln_sum[2], s.fb)
                        nc.gpsimd.tensor_tensor(x2b[:], x2, ffb[:].unsqueeze(1).broadcast_to([P, NT, D]),
                                                ALU.add).then_inc(x2b_done, 1)
                    if s.project:
                        for e in PICK_SLOTS.get(c, ()):
                            pick_expert(s, e)
                        for n in TREE_SLOTS.get(c, ()):
                            sum_gates(s, n)
                        if c == SPLIT_SLOT:
                            split_gates(s)
                    if s.finish and c == RSTD2_SLOT:
                        rstd(2, s.fb)
                    if s.attend and c == RSTD0_SLOT:
                        rstd(0, s.ab)
                    if s.experts and c % 2 == 1 and c not in POOL_FIRST:
                        low_part(s, c)

            pipeline(pool, step)

        @block.scalar
        def _(act):
            act.wait_ge(s_first, 16)

            def high_parts(dst, n):
                act.wait_ge(s_raw[n], 16)
                nc.scalar.activation(dst[:, WH * (n % 2):WH * (n % 2 + 1)].rearrange("p (c d) -> p c d", d=D),
                                     w_raw[:, n % 2, :, :], ACT.Copy).then_inc(s_seta, 1)

            def setup():
                high_parts(win_h, 0)
                high_parts(win_h, 1)

            def setup_more():
                high_parts(wout_h, 2)
                high_parts(wout_h, 3)

            def setup_logs():
                act.wait_ge(s_set, 8)
                nc.scalar.activation(choice[:, 3, :], choice[:, 2, :], ACT.Exp, accum_out=pick[:, 1:2]).then_inc(s_seta, 1)
                act.wait_ge(s_seta, 5)
                nc.scalar.activation(pick[:, 2:3], pick[:, 1:2], ACT.Ln).then_inc(s_seta, 1)
                nc.scalar.activation(choice[:, 4, :], choice_in[:, 1, :], ACT.Ln).then_inc(s_seta, 1)
                act.wait_ge(s_seta, 7)
                nc.scalar.activation(choice[:, 5, :], choice[:, 4, :], ACT.Ln, scale=-1.0).then_inc(s_seta, 1)

            def high(psum, dst, bias, full, free, b, done):
                act.wait_ge(full, b + 1)
                if due(192 * b):
                    act.wait_ge(free, 192 * b)
                nc.scalar.activation(dst[:], psum[:], ACT.Identity, bias=bias[:, 0:1]).then_inc(done, 1)

            def keep_gate(s, e):
                act.wait_ge(pe_gate, E * s.ab + e + 1)
                if e == 0:
                    if due(NC * (s.ab - 1)):
                        act.wait_ge(hid_done, NC * (s.ab - 1))
                nc.scalar.activation(gates[:, s.au, e, :], ps_gate[:], ACT.Copy).then_inc(gates_done, 1)

            def keep_rows(s):
                act.wait_ge(pe_rows, s.ab + 1)
                if due(E * s.ab):
                    act.wait_ge(pe_gate, E * s.ab)
                nc.scalar.activation(gate_rows[0:GROWS, :], ps_gate[0:GROWS, :], ACT.Copy).then_inc(rows_done, 1)

            def exps(s, j):
                act.wait_ge(pe_logit, 8 * s.ab + j + 1)
                if j % 2 == 0:
                    if due(NT * s.ab + j // 2 - 1):
                        act.wait_ge(pe_pv, NT * s.ab + j // 2 - 1)
                nc.scalar.activation(probs[:, j // 2 % 2, :, j % 2, :], ps_score[j % 2][:].rearrange("p (m q) -> p m q", q=L),
                                     ACT.Exp, scale=SCALE).then_inc(exp_done, 1)

            def scale_out(n, b, dst):
                act.wait_ge(ln_shifted[n], b + 1)
                for j in range(NT):
                    last = nc.scalar.activation(dst[:, j, :], ln_x[:, n, j, :], ACT.Identity,
                                                bias=ln_shift[:, n, j:j + 1], scale=ln_rs[:, n, j:j + 1])
                last.then_inc(ln_out[n], 1)

            def k_head(s, n):
                h, g = n // 2, slice(2 * (n % 2), 2 * (n % 2) + 2)
                if n == 0:
                    act.wait_ge(kstack_in, 192 * (s.pb + 1))
                    if due(8 * s.pb):
                        act.wait_ge(pe_score, 8 * s.pb)
                ins = nc.scalar.activation(k_heads[0:ROWS, g, h, :], k_stack[0:ROWS, s.pu, g, :], ACT.Copy,
                                           scale=headmask[0:ROWS, h:h + 1])
                if n == 2 * HG - 1 or s.fixed == -2 and n == FIRST_KHEADS - 1:
                    ins.then_inc(kheads_done, 1)

            def high_part(s, c):
                act.wait_ge(hid_done, NC * s.eb + c + 1)
                if due(NC * s.eb + c + 1 - HP):
                    act.wait_ge(pe_moe, NC * s.eb + c + 1 - HP)
                nc.scalar.activation(hid_h[:, c % HP, :], hid[:, c % HB, :], ACT.Copy).then_inc(high_done, 1)

            def step(s):
                if s.attend:
                    act.wait_ge(pe_maxt, s.ab + 1)
                    if due(32 * s.ab):
                        act.wait_ge(max_in, 32 * s.ab)
                    nc.scalar.activation(mh[:], ps_pf[0:H, :], ACT.Copy, scale=1.0 / MAXSCALE).then_inc(mh_done, 1)
                for c in range(SLOTS):
                    if s.experts and c not in HIGH_LAST:
                        high_part(s, c)
                    if s.finish and c == 0:
                        act.wait_ge(pe_moe, NC * (s.fb + 1))
                        if due(s.fb):
                            act.wait_ge(pe_ffn, s.fb)
                        nc.scalar.activation(turned[:], ps_moe[:], ACT.Copy).then_inc(moe_done, 1)
                    if s.attend and c == ROWS_SLOT:
                        keep_rows(s)
                    if s.queries and c == Q_SLOT:
                        high(ps_pf, qh, bqs, pe_q, qstack_in, s.qb, qh_done)
                    if s.queries and c == K_SLOT:
                        high(ps_pf, kh, bks, pe_k, kstack_in, s.qb, kh_done)
                    if s.finish and c == X2_SLOT:
                        scale_out(1, s.fb, x2)
                    if s.finish and c == X2T_SLOT:
                        act.wait_ge(pe_x2t, s.fb + 1)
                        act.wait_ge(pe_moet, s.fb + 1)
                        nc.scalar.activation(turned[:], ps_pf[:], ACT.Copy).then_inc(x2t_done, 1)
                    if s.attend:
                        for j in (FIRST_LOGIT_SLOTS if s.fixed == -1 else LOGIT_SLOTS).get(c, ()):
                            exps(s, j)
                    if s.attend and c == OT_SLOT:
                        act.wait_ge(pe_ot, s.ab + 1)
                        if due(s.ab):
                            act.wait_ge(pe_op, s.ab)
                        nc.scalar.activation(o_t[:], ps_at[:], ACT.Copy).then_inc(ot_done, 1)
                    if s.finish and c == Y_SLOT:
                        scale_out(2, s.fb, y)
                    if s.attend and c == X1_SLOT:
                        scale_out(0, s.ab, x1[:, s.au, :, :])
                    if s.fixed == -1 and c == 5:
                        setup_more()
                    if s.fixed == -1 and c == 7:
                        setup_logs()
                    if s.attend:
                        for e in GATE_SLOTS.get(c, ()):
                            keep_gate(s, e)
                    if s.project:
                        for n in KHEAD_SLOTS.get(c, ()):
                            if not (s.fixed == -2 and n >= FIRST_KHEADS):
                                k_head(s, n)
                    if s.attend and c == 15:
                        act.wait_ge(pe_x1t, s.ab + 1)
                        nc.scalar.activation(x1h[:, s.au, :], ps_at[:], ACT.Copy).then_inc(x1h_done, 1)
                    if s.experts and c in HIGH_LAST:
                        high_part(s, c)

            pipeline(act, step, after_second=setup)

        @block.vector
        def _(dve):
            nc.vector.memset(k_stack[ROWS:MROWS, :, :, :], -MAXSCALE)
            dve.wait_ge(s_first, 16)
            dec = decay.rearrange("p (h m) -> p h m", h=2)
            count = [0]

            def did(ins):
                count[0] += 1
                ins.then_inc(s_set, 1)
                dve.wait_ge(s_set, count[0])

            def need_rest():
                dve.wait_ge(s_rest, 16)
                dve.wait_ge(s_setp, 3)

            def low_parts(low_part, high_part, n):
                half = slice(WH * (n % 2), WH * (n % 2 + 1))
                dve.wait_ge(s_seta, n + 1)
                did(nc.vector.tensor_tensor(low_part[:, half].rearrange("p (c d) -> p c d", d=D), w_raw[:, n % 2, :, :],
                                            high_part[:, half].rearrange("p (c d) -> p c d", d=D).bitcast(F32), ALU.subtract))

            def setup():
                nc.vector.memset(pick[:], 0.0)
                for n in range(2):
                    low_parts(win_l, win_h, n)
                for par in range(2):
                    for j in range(NT):
                        for b in range(2):
                            r = slice(L * b, L * b + L)
                            nc.vector.tensor_copy(vals_v[r, par, j, b, :, :, HD], dec[r])
                nc.vector.tensor_copy(ident_b[:], ident)
                did(nc.vector.tensor_copy(select[:], expertmask.unsqueeze(2).broadcast_to([P, E, P])))

            def setup_more():
                for n in range(2, 4):
                    low_parts(wout_l, wout_h, n)
                dve.wait_ge(s_rows, 16)
                dve.wait_ge(s_sett, 1)
                did(nc.vector.tensor_tensor(attn_bias, ps_moe[:, 0:D], attn_bias, ALU.add))

            def setup_choice():
                did(nc.vector.tensor_reduce(pick[:, 0:1], choice_in[:, 0, :], AX.X, ALU.max))
                did(nc.vector.tensor_scalar(choice[:, 2, :], choice_in[:, 0, :], pick[:, 0:1], None, ALU.subtract))
                dve.wait_ge(s_seta, 8)
                did(nc.vector.tensor_scalar(choice[:, 6, :], choice[:, 2, :], pick[:, 2:3], None, ALU.subtract))
                did(nc.vector.tensor_tensor(choice[:, 7, :], choice[:, 6, :], choice[:, 5, :], ALU.subtract))
                did(nc.vector.tensor_reduce(pick[:, 3:4], choice[:, 7, :], AX.X, ALU.max))
                did(nc.vector.tensor_scalar(choice[:, 8, :], choice[:, 7, :], pick[:, 3:4], float(NOPS), ALU.is_lt, ALU.mult))
                did(nc.vector.tensor_tensor(choice[:, 9, :], choice[:, 8, :], iota, ALU.add))
                did(nc.vector.tensor_reduce(pick[:, 4:5], choice[:, 9, :], AX.X, ALU.min))
                did(nc.vector.tensor_scalar(choice[:, 10, :], iota, pick[:, 4:5], None, ALU.is_equal))

            def setup_ffn():
                dve.wait_ge(s_ffw, 32)
                for n in range(NOPS):
                    for dst, src in ((ffw, ffw_all), (ffb, ffb_all)):
                        if n == 0:
                            did(nc.vector.tensor_scalar(dst[:], src[:, 0, :], choice[:, 10, 0:1], None, ALU.mult))
                        else:
                            did(nc.vector.scalar_tensor_tensor(out=dst[:], in0=src[:, n, :], scalar=choice[:, 10, n:n + 1],
                                                               in1=dst[:], op0=ALU.mult, op1=ALU.add))

            def low(psum, dst, high, bias, ready, b, done):
                dve.wait_ge(ready, b + 1)
                nc.vector.scalar_tensor_tensor(out=dst[:], in0=psum[:], scalar=bias[:, 0:1], in1=high[:],
                                               op0=ALU.add, op1=ALU.subtract).then_inc(done, 1)

            def keep_vals(s):
                dve.wait_ge(pe_v, s.pb + 1)
                if due(NT * (s.pb - 1)):
                    dve.wait_ge(pe_pv, NT * (s.pb - 1))
                for j in range(NT):
                    v = ps_pf[:, P * j:P * (j + 1)].rearrange("p (h m x) -> p h m x", h=2, x=HD)
                    for b in range(2):
                        r = slice(L * b, L * b + L)
                        last = nc.vector.tensor_tensor(vals_v[r, s.pu, j, b, :, :, 0:HD], v[r],
                                                       dec[r].unsqueeze(3).broadcast_to([L, 2, H // 2, HD]), ALU.mult)
                last.then_inc(vals_done, 1)

            def maximum(b, j):
                dve.wait_ge(pe_score, 8 * b + j + 1)
                if j == 0:
                    if due(b):
                        dve.wait_ge(pe_maxt, b)
                nc.vector.tensor_reduce(smax[:, j // 2, 8 * (j % 2):8 * (j % 2) + 8],
                                        ps_score[j % 2][:].rearrange("p (h k) -> p h k", k=L), AX.X,
                                        ALU.max).then_inc(max_done, 1)

            def normalise(s, j):
                dve.wait_ge(pe_pv, NT * s.ab + j + 1)
                acc = ps_at[:, 0:H // 2 * VC].rearrange("p (m q x) -> p m q x", q=4, x=HD + 1)
                nc.vector.reciprocal(rden[:], acc[:, :, :, HD]).then_inc(rden_done, 1)
                if j == 0:
                    if due(s.ab):
                        dve.wait_ge(pe_ot, s.ab)
                dve.wait_ge(rden_done, NT * s.ab + j + 1)
                for h2 in range(2):
                    for b in range(2):
                        q = 2 * h2 + b
                        r = slice(L * h2, L * h2 + L)
                        dst = o_tok[L * b:L * b + L, j, 64 * h2:64 * h2 + 64].rearrange("p (m x) -> p m x", x=HD)
                        last = nc.vector.tensor_tensor(dst, acc[r, :, q, 0:HD],
                                                       rden[r, :, q].unsqueeze(2).broadcast_to([L, H // 2, HD]), ALU.mult)
                last.then_inc(otok_done, 1)

            def first_k_heads(s):
                dve.wait_ge(kstack_in, 192)
                for n in range(FIRST_KHEADS, 2 * HG):
                    h, g = n // 2, slice(2 * (n % 2), 2 * (n % 2) + 2)
                    last = nc.vector.tensor_scalar(k_heads[0:ROWS, g, h, :], k_stack[0:ROWS, s.pu, g, :],
                                                   headmask[0:ROWS, h:h + 1], None, ALU.mult)
                last.then_inc(first_kheads, 1)

            def q_head(s, n):
                h, pair = n % HG, n // HG
                if n == 0:
                    dve.wait_ge(qstack_in, 192 * (s.pb + 1))
                if h == 0:
                    if due(8 * s.ab + 4 * pair + 4):
                        dve.wait_ge(pe_logit, 8 * s.ab + 4 * pair + 4)
                tok = slice(2 * P * pair, 2 * P * pair + 2 * P)
                ins = nc.vector.tensor_scalar(q_heads[0:ROWS, :, h, tok], q_stack[0:ROWS, s.pu, :, tok],
                                              headmask[0:ROWS, h:h + 1], None, ALU.mult)
                if n == 2 * HG - 1:
                    ins.then_inc(qheads_done, 1)

            def stats(n, b):
                dve.wait_ge(ln_sum[n], b + 1)
                for j in range(NT):
                    last = nc.vector.bn_stats(ln_st[:, n, j, :], ln_x[:, n, j, :])
                last.then_inc(ln_stat[n], 1)

            def variance(n, b):
                for j in range(NT):
                    last = nc.vector.bn_aggr(ln_mv[:, n, j, :], ln_st[:, n, j, :])
                last.then_inc(ln_var[n], 1)

            def add_eps(n, b):
                dve.wait_ge(ln_var[n], b + 1)
                nc.vector.tensor_scalar(ln_ve[:, n, :], ln_mv[:, n, :, 1], EPS, None, ALU.add).then_inc(ln_eps[n], 1)

            def shift(n, b):
                dve.wait_ge(ln_rstd[n], b + 1)
                nc.vector.scalar_tensor_tensor(out=ln_shift[:, n, :], in0=ln_mv[:, n, :, 0], scalar=-1.0, in1=ln_rs[:, n, :],
                                               op0=ALU.mult, op1=ALU.mult).then_inc(ln_shifted[n], 1)

            def low_part(s, c):
                dve.wait_ge(high_done, NC * s.eb + c + 1)
                if due(NC * s.eb + c + 1 - HB):
                    dve.wait_ge(pe_moe, NC * s.eb + c + 1 - HB)
                nc.vector.tensor_tensor(hid_l[:, c % HB, :], hid[:, c % HB, :],
                                        hid_h[:, c % HP, :].bitcast(F32), ALU.subtract).then_inc(low_even, 1)

            def step(s):
                for c in range(SLOTS):
                    if s.finish and c == VAR1_SLOT:
                        dve.wait_ge(ln_stat[1], s.fb + 1)
                    if s.finish and c == STAT_SLOT + 1:
                        dve.wait_ge(ln_stat[2], s.fb + 1)
                    if s.attend and c == WO_SLOT + 1:
                        dve.wait_ge(ln_stat[0], s.ab + 1)
                    if s.experts:
                        dve.wait_ge(pe_hid, NC * s.eb + c + 1)
                        if c % 2 == 0:
                            dve.wait_ge(gates_done, E * s.eb + c // 2 + 1)
                        if due(NC // 2 * s.eb + c // 2):
                            dve.wait_ge(low_odd if c % 2 else low_even, NC // 2 * s.eb + c // 2)
                        nc.vector.scalar_tensor_tensor(out=hid[:, c % HB, :], in0=ps_hid[c % 2][:], scalar=0.0,
                                                       in1=gates[:, s.eu, c // 2, :], op0=ALU.max,
                                                       op1=ALU.mult).then_inc(hid_done, 1)
                    if s.finish and c == VAR1_SLOT:
                        variance(1, s.fb)
                        add_eps(1, s.fb)
                    if s.finish and c == STAT_SLOT + 1:
                        variance(2, s.fb)
                        add_eps(2, s.fb)
                    if s.attend and c == WO_SLOT + 1:
                        variance(0, s.ab)
                        add_eps(0, s.ab)
                    if s.attend and c == SHIFT0_SLOT:
                        shift(0, s.ab)
                    if s.experts and c % 2 == 1 and c not in LOW_LAST:
                        low_part(s, c - 1)
                    if s.attend and c == 0:
                        dve.wait_ge(mh_done, s.ab + 1)
                        nc.vector.scalar_tensor_tensor(out=ml[:], in0=ps_pf[0:H, :], scalar=1.0 / MAXSCALE, in1=mh[:],
                                                       op0=ALU.mult, op1=ALU.subtract).then_inc(ml_done, 1)
                    if s.finish and c == 1:
                        dve.wait_ge(pe_moet, s.fb + 1)
                        nc.vector.tensor_tensor(ln_x[:, 1, :, :], ps_gate[:].rearrange("p (j d) -> p j d", d=D),
                                                x1[:, s.fu, :, :], ALU.add).then_inc(ln_sum[1], 1)
                    if s.finish and c == 1:
                        stats(1, s.fb)
                    if s.fixed == -2 and c == V_SLOT:
                        first_k_heads(s)
                    if s.project and c == V_SLOT:
                        keep_vals(s)
                    if s.fixed == -1 and c in (5, 7, 9):
                        (setup_more if c == 5 else setup_choice if c == 7 else setup_ffn)()
                    if s.finish and c == SHIFT1_SLOT:
                        shift(1, s.fb)
                    if s.attend and c in NORM_SLOTS:
                        normalise(s, NORM_SLOTS[c])
                    if s.finish and c == SUM_SLOT:
                        dve.wait_ge(pe_ffn, s.fb + 1)
                        if due(16 * s.fb):
                            dve.wait_ge(stored, 16 * s.fb)
                        dve.wait_ge(x2b_done, s.fb + 1)
                        nc.vector.tensor_tensor(ln_x[:, 2, :, :], ps_pf[:].rearrange("p (j d) -> p j d", d=D),
                                                x2b[:], ALU.add).then_inc(ln_sum[2], 1)
                    if s.finish and c == STAT_SLOT:
                        stats(2, s.fb)
                    if s.queries and c == QL_SLOT:
                        low(ps_pf, ql, qh, bqs, qh_done, s.qb, ql_done)
                    if s.queries and c == KL_SLOT:
                        low(ps_pf, kl, kh, bks, kh_done, s.qb, kl_done)
                    if s.project:
                        for n in QHEAD_SLOTS.get(c, ()):
                            q_head(s, n)
                        for j in MAX_SLOTS.get(c, ()):
                            maximum(s.pb, j)
                    if s.finish and c == SHIFT_SLOT:
                        shift(2, s.fb)
                    if s.attend and c == WO_SLOT:
                        dve.wait_ge(pe_op, s.ab + 1)
                        dve.wait_ge(xb_done, s.ab + 1)
                        nc.vector.tensor_tensor(ln_x[:, 0, :, :], ps_at[:].rearrange("p (j d) -> p j d", d=D),
                                                xtok[:, s.au, :, :], ALU.add).then_inc(ln_sum[0], 1)
                        stats(0, s.ab)
                    if s.attend and c == 15:
                        dve.wait_ge(x1h_done, s.ab + 1)
                        nc.vector.tensor_tensor(x1l[:, s.au, :], ps_at[:], x1h[:, s.au, :].bitcast(F32),
                                                ALU.subtract).then_inc(x1l_done, 1)
                    if s.experts and c % 2 == 1 and c in LOW_LAST:
                        low_part(s, c - 1)

            pipeline(dve, step, need_rest, setup)

        @block.tensor
        def _(pe):
            pe.wait_ge(s_first, 16)

            def need_rest():
                pe.wait_ge(s_rest, 16)

            def setup():
                nc.tensor.matmul(ps_moe[:, 0:D], bvs[:, 0:1].broadcast_to([P, P]), wo, start=True, stop=True).then_inc(s_sett, 1)
                pe.wait_ge(s_set, 3)

            def hidden(s, c):
                if c == 0:
                    pe.wait_ge(x1h_done, s.eb + 1)
                    pe.wait_ge(x1l_done, s.eb + 1)
                if due(NC * s.eb + c - 1):
                    pe.wait_ge(hid_done, NC * s.eb + c - 1)
                w = slice(P * c, P * (c + 1))
                nc.tensor.matmul(ps_hid[c % 2][:], win_h[:, w], x1h[:, s.eu, :], start=True, stop=False)
                nc.tensor.matmul(ps_hid[c % 2][:], win_l[:, w], x1h[:, s.eu, :], start=False, stop=False)
                nc.tensor.matmul(ps_hid[c % 2][:], win_h[:, w], x1l[:, s.eu, :], start=False, stop=True).then_inc(pe_hid, 1)

            def expert_out(b, c):
                pe.wait_ge(high_done, NC * b + c + 1)
                if c == 0:
                    if due(b):
                        pe.wait_ge(moe_done, b)
                w = slice(D * c, D * (c + 1))
                nc.tensor.matmul(ps_moe[:], wout_h[:, w], hid_h[:, c % HP, :], start=(c == 0), stop=False)
                nc.tensor.matmul(ps_moe[:], wout_l[:, w], hid_h[:, c % HP, :], start=False, stop=False)
                pe.wait_ge(low_odd if c % 2 else low_even, NC // 2 * b + c // 2 + 1)
                nc.tensor.matmul(ps_moe[:], wout_h[:, w], hid_l[:, c % HB, :], start=False,
                                 stop=(c == NC - 1)).then_inc(pe_moe, 1)

            def tiles_t(dst, src, done):
                for j in range(NT):
                    last = nc.tensor.transpose(dst[:, P * j:P * (j + 1)], src(j), ident)
                last.then_inc(done, 1)

            def score(b, par, j):
                if j == 0:
                    pe.wait_ge(kheads_done, b + 1)
                    if isinstance(b, int) and b == 0:
                        pe.wait_ge(first_kheads, 1)
                    pe.wait_ge(qstack_in, 192 * (b + 1))
                if j < 2:
                    if due(8 * b - 1 + j):
                        pe.wait_ge(exp_done, 8 * b - 1 + j)
                else:
                    pe.wait_ge(max_done, 8 * b + j - 1)
                for g in (2 * (j % 2), 2 * (j % 2) + 1):
                    for h in range(2):
                        tok = slice(P * (j // 2) + L * h, P * (j // 2) + L * h + L)
                        last = nc.tensor.matmul(ps_score[j % 2][L * h:L * h + L, 256 * (g % 2):256 * (g % 2) + 256],
                                                q_stack[0:ROWS, par, g, tok], k_heads[0:ROWS, g, :, tok],
                                                start=True, stop=True)
                last.then_inc(pe_score, 1)

            def logit(s, j):
                if j == 0:
                    pe.wait_ge(max_in, 32 * (s.ab + 1))
                    pe.wait_ge(qheads_done, s.ab + 1)
                if j < 2:
                    pe.wait_ge(max_done, 8 * s.ab + 7 + j)
                else:
                    pe.wait_ge(exp_done, 8 * s.ab + j - 1)
                for g in (2 * (j % 2), 2 * (j % 2) + 1):
                    for b in range(2):
                        tok = slice(P * (j // 2) + L * b, P * (j // 2) + L * b + L)
                        last = nc.tensor.matmul(ps_score[j % 2][L * b:L * b + L, 256 * (g % 2):256 * (g % 2) + 256],
                                                k_stack[0:MROWS, s.au, g, tok], q_heads[0:MROWS, g, :, tok],
                                                start=True, stop=True)
                last.then_inc(pe_logit, 1)

            def weigh(s, j):
                pe.wait_ge(exp_done, 8 * s.ab + 2 * j + 2)
                if j == 0:
                    pe.wait_ge(vals_done, s.ab + 1)
                    if due(s.ab):
                        pe.wait_ge(x1l_done, s.ab)
                else:
                    pe.wait_ge(otok_done, NT * s.ab + j)
                for m in range(H // 2):
                    last = nc.tensor.matmul(ps_at[:, VC * m:VC * (m + 1)], probs[:, j % 2, m, :, :].rearrange("p n q -> p (n q)"),
                                            vals[:, s.au, j, m, :], start=True, stop=True)
                last.then_inc(pe_pv, 1)

            def gate_to_rows(s):
                pe.wait_ge(gate_done, s.ab + 1)
                if s.finish:
                    pe.wait_ge(ln_sum[1], s.fb + 1)
                if due(E * s.ab):
                    pe.wait_ge(gates_done, E * s.ab)
                for j in range(NT):
                    last = nc.tensor.matmul(ps_gate[0:GROWS, P * j:P * (j + 1)],
                                            gate_parts[:, j, :, :].rearrange("p n e -> p (n e)"), ident_b[:], start=True, stop=True)
                last.then_inc(pe_rows, 1)

            def spread_gate(s, e):
                if e == 0:
                    pe.wait_ge(rows_done, s.ab + 1)
                if due(E * s.ab + e):
                    pe.wait_ge(gates_done, E * s.ab + e)
                nc.tensor.matmul(ps_gate[:], select[0:GROWS, e, :], gate_rows[0:GROWS, :], start=True, stop=True).then_inc(pe_gate, 1)

            def step(s):
                if s.finish:
                    expert_out(s.fb, NC - 2)
                if s.attend:
                    pe.wait_ge(max_done, 8 * (s.ab + 1))
                    if due(s.fb):
                        pe.wait_ge(ln_sum[2], s.fb)
                    if s.project:
                        pe.wait_ge(ql_done, s.pb + 1)
                    for j in range(NT):
                        last = nc.tensor.transpose(ps_pf[0:H, P * j:P * (j + 1)], smax[:, j, :], ident)
                    last.then_inc(pe_maxt, 1)
                if s.experts:
                    if s.fixed == 0:
                        pe.wait_ge(s_set, SETUP_B)
                    hidden(s, 0)
                for c in range(SLOTS):
                    if s.experts and c + 1 < NC:
                        hidden(s, c + 1)
                    if s.experts and c in EO_FIRST:
                        expert_out(s.eb, c - 2)
                    if s.finish and c == 0:
                        expert_out(s.fb, NC - 1)
                    if s.finish and c == 1:
                        pe.wait_ge(moe_done, s.fb + 1)
                        pe.wait_ge(gates_done, E * (min(s.ab, NB) if isinstance(s.t, int) else s.ab))
                        tiles_t(ps_gate, lambda j: turned[:, P * j:P * (j + 1)], pe_moet)
                    if s.queries and c == K_SLOT:
                        pe.wait_ge(ld_xt[s.qu], 16 * s.qh + 16)
                        if s.project:
                            pe.wait_ge(vals_done, s.pb + 1)
                        if due(s.fb + 1):
                            pe.wait_ge(ln_sum[2], s.fb + 1)
                        nc.tensor.matmul(ps_pf[:], wk, xt[:, s.qu, :], start=True, stop=True).then_inc(pe_k, 1)
                    if s.queries and c == Q_SLOT:
                        pe.wait_ge(kl_done, s.qb + 1)
                        nc.tensor.matmul(ps_pf[:], wq, xt[:, s.qu, :], start=True, stop=True).then_inc(pe_q, 1)
                    if s.project and c == V_SLOT:
                        pe.wait_ge(ql_done, s.pb + 1)
                        if s.attend:
                            pe.wait_ge(ml_done, s.ab + 1)
                        for j in range(NT):
                            last = nc.tensor.matmul(ps_pf[:, P * j:P * (j + 1)], xt[:, s.pu, P * j:P * (j + 1)],
                                                    wv, start=True, stop=True)
                        last.then_inc(pe_v, 1)
                    if s.finish and c == X2T_SLOT:
                        pe.wait_ge(ln_out[1], s.fb + 1)
                        if s.project:
                            pe.wait_ge(vals_done, s.pb + 1)
                        else:
                            pe.wait_ge(vals_done, NB)
                            if s.attend:
                                pe.wait_ge(ml_done, s.ab + 1)
                            pe.wait_ge(ln_sum[2], s.fb)
                        tiles_t(ps_pf, lambda j: x2[:, j, :], pe_x2t)
                    if s.finish and c == FFN_SLOT:
                        pe.wait_ge(x2t_done, s.fb + 1)
                        for j in range(NT):
                            last = nc.tensor.matmul(ps_pf[:, P * j:P * (j + 1)], turned[:, P * j:P * (j + 1)],
                                                    ffw[:], start=True, stop=True)
                        last.then_inc(pe_ffn, 1)
                    if s.attend:
                        for j in (FIRST_LOGIT_SLOTS if s.fixed == -1 else LOGIT_SLOTS).get(c, ()):
                            logit(s, j)
                    if s.attend and c in WEIGH_SLOTS:
                        weigh(s, WEIGH_SLOTS[c])
                    if s.attend and c == OT_SLOT:
                        pe.wait_ge(otok_done, NT * (s.ab + 1))
                        tiles_t(ps_at, lambda j: o_tok[:, j, :], pe_ot)
                    if s.attend and c == WO_SLOT:
                        pe.wait_ge(ot_done, s.ab + 1)
                        for j in range(NT):
                            last = nc.tensor.matmul(ps_at[:, P * j:P * (j + 1)], o_t[:, P * j:P * (j + 1)],
                                                    wo, start=True, stop=True)
                        last.then_inc(pe_op, 1)
                    if s.attend and c == ROWS_SLOT:
                        gate_to_rows(s)
                    if s.attend:
                        for e in GATE_SLOTS.get(c, ()):
                            spread_gate(s, e)
                    if s.project:
                        for j in SCORE_SLOTS.get(c, ()):
                            score(s.pb, s.pu, j)
                    if s.experts and c == NC - 1:
                        expert_out(s.eb, c - 2)
                    if s.attend and c == 15:
                        pe.wait_ge(ln_out[0], s.ab + 1)
                        tiles_t(ps_at, lambda j: x1[:, s.au, j, :], pe_x1t)
                    if s.experts and 1 < c < NC - 1 and c not in EO_FIRST:
                        expert_out(s.eb, c - 2)

            pipeline(pe, step, need_rest, setup)


def build(nc, shapes, out_shape):
    args = [nc.dram_tensor(f"in_{name}", list(shape), dt, kind="ExternalInput").ap() for name, shape, dt in shapes]
    out = nc.dram_tensor("out_0", list(out_shape), F32, kind="ExternalOutput").ap()
    decoder_layer(nc, *args, out)


def kernel(x, ctx_512, itok_BxS2xS_0_7, L0_attn_Wq, L0_attn_bq, L0_attn_Wk, L0_attn_bk, L0_attn_Wv, L0_attn_bv,
           L0_attn_Wo, L0_attn_bo, L0_xattn_proj_in, L0_xattn_proj_out, L0_ffn_W, L0_ffn_b, L0_ffn_logits, L0_ffn_u):
    import concourse.bacc as bacc
    from concourse.bass_utils import run_bass_kernel_spmd

    def tiles(a):
        return np.ascontiguousarray(np.asarray(a).reshape(NB, NT, P, -1).transpose(0, 2, 1, 3))

    def con(a):
        return np.ascontiguousarray(a)

    x = np.asarray(x)
    slopes = np.power(np.float32(2.0), np.linspace(-4.0, -0.3, H, dtype=np.float32))
    decay = np.exp(-(np.arange(L, dtype=np.float64)[:, None] * slopes[None, :].astype(np.float64))).astype(np.float32)
    headmask = (np.arange(P)[:, None] % TERM // HD == np.arange(HG)[None, :]).astype(np.float32)
    expertmask = (np.arange(P)[:, None] % 32 == np.arange(E)[None, :]).astype(np.float32)
    arrays = {
        "x_tok": tiles(x.reshape(B * L, D)),
        "x_t": con(x.reshape(NB, BLK, D).transpose(0, 2, 1)),
        "gate_w": tiles(np.asarray(ctx_512).transpose(0, 2, 1).reshape(B * L, K)),
        "gate_e": tiles(np.asarray(itok_BxS2xS_0_7).transpose(0, 2, 1).reshape(B * L, K)),
        "first": con(np.concatenate([np.asarray(L0_attn_Wk).T, np.asarray(L0_attn_Wq).T, np.asarray(L0_attn_bk).reshape(D, 1),
                                     np.asarray(L0_attn_bq).reshape(D, 1), headmask], axis=1)),
        "rest": con(np.concatenate([np.eye(P, dtype=np.float32), np.asarray(L0_attn_Wv).T, np.asarray(L0_attn_Wo).T,
                                    np.asarray(L0_attn_bv).reshape(D, 1), np.concatenate([decay, decay]), expertmask,
                                    np.broadcast_to(np.arange(NOPS, dtype=np.float32), (P, NOPS))], axis=1)),
        "rows": con(np.concatenate([np.asarray(a).reshape(1, -1) for a in
                                    (L0_attn_bo, L0_ffn_logits, L0_ffn_u)], axis=1)),
        "w_in": con(np.asarray(L0_xattn_proj_in).reshape(E * DH, D).T),
        "w_out": con(np.asarray(L0_xattn_proj_out).transpose(0, 2, 1).reshape(NC, P, D).transpose(1, 0, 2).reshape(P, NC * D)),
        "ffn_w": con(np.asarray(L0_ffn_W).transpose(1, 0, 2)), "ffn_b": con(np.asarray(L0_ffn_b).reshape(1, NOPS, D)),
    }
    nc = bacc.Bacc("TRN2", target_bir_lowering=False, num_devices=1)
    build(nc, [(n, a.shape, mybir.dt.from_np(a.dtype)) for n, a in arrays.items()], (NB, P, NT, D))
    r = run_bass_kernel_spmd(nc, [{f"in_{n}": a for n, a in arrays.items()}], core_ids=[0])
    y = r.results[0]["out_0"]
    return con(y.transpose(0, 2, 1, 3)).reshape(B, L, D)
```
